# Optimizing a Trainium2 kernel written in Bass

```python
import numpy as np
import jax
import jax.numpy as jnp

def _softmax(x, axis=-1):
    return jax.nn.softmax(x, axis=axis)

def _gelu(x):
    return jax.nn.gelu(x, approximate=True)

def _silu(x):
    return jax.nn.silu(x)

def _sigmoid(x):
    return jax.nn.sigmoid(x)

def _layernorm(x, axis=-1, eps=1e-05):
    m = jnp.mean(x, axis=axis, keepdims=True)
    v = jnp.var(x, axis=axis, keepdims=True)
    return (x - m) / jnp.sqrt(v + eps)

def _scatter_add(tgt, idx, src, axis=0):
    return tgt.at[idx].add(src)

def _segment_sum(src, seg, n):
    return jax.ops.segment_sum(src, seg, n)
kernel_name = 'mk_adj_ffn_d1_adj_r2_e4a65a'

def setup_inputs(seed: int=0):
    np.random.seed(seed)
    _w = jnp.asarray

    def _rec_inputs():
        import jax
        import jax.numpy as jnp
        _gk = jax.random.key(seed)
        x = -0.0005207 + 1.001 * jax.random.normal(jax.random.fold_in(_gk, 1), (4096, 128), jnp.float32)
        _w = (1.0 + jnp.arange(4096, dtype=jnp.float32)) ** (-0.5)
        _w = _w / _w.mean()
        _pij = jnp.clip(0.00195312 * _w[:, None] * _w[None, :], 0.0, 1.0)
        _a = jax.random.uniform(jax.random.fold_in(_gk, 2), (4096, 4096)) < _pij
        _a = jnp.logical_or(_a, jnp.eye(4096, dtype=bool))
        _af = _a.astype(jnp.float32)
        _af = _af * jax.random.uniform(jax.random.fold_in(_gk, 3), (4096, 4096), jnp.float32, 0.05, 1)
        adj = _af
        return (x, adj)
    x, adj = _rec_inputs()

    def _L0_gnn_setup():
        import jax, jax.numpy as jnp
        import numpy as np
        N = 4096
        D = 128
        L = 3

        def _cxin_conv(x, a, eps, W, b):
            ax = a @ x
            h = ax + (1.0 + eps[0]) * ax
            for i in range(L):
                h = jax.nn.relu(h @ W[i].T + b[i])
            return h
        key = jax.random.key(seed)
        ks = jax.random.split(key, 8)
        s = 1.0 / np.sqrt(D)
        return {'x1': jax.random.normal(ks[0], (N, D), jnp.float32), 'x2': jax.random.normal(ks[1], (N, D), jnp.float32), 'G1': jax.random.uniform(ks[2], (N, N), jnp.float32), 'G2': jax.random.uniform(ks[3], (N, N), jnp.float32), 'eps1': jnp.zeros((1,), jnp.float32), 'eps2': jnp.zeros((1,), jnp.float32), 'W1': jax.random.normal(ks[4], (L, D, D), jnp.float32) * s, 'b1': jnp.zeros((L, D), jnp.float32), 'W2': jax.random.normal(ks[5], (L, D, D), jnp.float32) * s, 'b2': jnp.zeros((L, D), jnp.float32), 'Wm': jax.random.normal(ks[6], (D, 2 * D), jnp.float32) * (1.0 / np.sqrt(2 * D)), 'bm': jnp.zeros((D,), jnp.float32)}
    _L0_gnn_all = _L0_gnn_setup()
    _L0_gnn_in = {k: v for k, v in _L0_gnn_all.items() if k in ('x2', 'eps1', 'eps2', 'W1', 'b1', 'W2', 'b2', 'Wm', 'bm')}
    del _L0_gnn_all

    def _L0_ffn_setup():
        import jax, jax.numpy as jnp
        import numpy as np
        B, S, D, H, E, K = (8, 4096, 128, 512, 8, 2)
        key = jax.random.key(seed)
        ks = jax.random.split(key, 7)
        s_in = 1.0 / np.sqrt(D)
        s_hid = 1.0 / np.sqrt(H)
        return {'x': jax.random.normal(ks[0], (B, S, D), dtype=jnp.float32), 'Wg': jax.random.uniform(ks[1], (E, D), jnp.float32, -s_in, s_in), 'bg': jax.random.uniform(ks[2], (E,), jnp.float32, -s_in, s_in), 'W1': jax.random.uniform(ks[3], (E, H, D), jnp.float32, -s_in, s_in), 'b1': jax.random.uniform(ks[4], (E, H), jnp.float32, -s_in, s_in), 'W2': jax.random.uniform(ks[5], (E, D, H), jnp.float32, -s_hid, s_hid), 'b2': jax.random.uniform(ks[6], (E, D), jnp.float32, -s_hid, s_hid)}
    _L0_ffn_all = _L0_ffn_setup()
    _L0_ffn_in = {k: v for k, v in _L0_ffn_all.items() if k in ('Wg', 'bg', 'W1', 'b1', 'W2', 'b2')}
    del _L0_ffn_all
    return {'x': x, 'adj': adj, 'L0_gnn_x2': _L0_gnn_in['x2'], 'L0_gnn_eps1': _L0_gnn_in['eps1'], 'L0_gnn_eps2': _L0_gnn_in['eps2'], 'L0_gnn_W1': _L0_gnn_in['W1'], 'L0_gnn_b1': _L0_gnn_in['b1'], 'L0_gnn_W2': _L0_gnn_in['W2'], 'L0_gnn_b2': _L0_gnn_in['b2'], 'L0_gnn_Wm': _L0_gnn_in['Wm'], 'L0_gnn_bm': _L0_gnn_in['bm'], 'L0_ffn_Wg': _L0_ffn_in['Wg'], 'L0_ffn_bg': _L0_ffn_in['bg'], 'L0_ffn_W1': _L0_ffn_in['W1'], 'L0_ffn_b1': _L0_ffn_in['b1'], 'L0_ffn_W2': _L0_ffn_in['W2'], 'L0_ffn_b2': _L0_ffn_in['b2']}

def reference(x, adj, L0_gnn_x2, L0_gnn_eps1, L0_gnn_eps2, L0_gnn_W1, L0_gnn_b1, L0_gnn_W2, L0_gnn_b2, L0_gnn_Wm, L0_gnn_bm, L0_ffn_Wg, L0_ffn_bg, L0_ffn_W1, L0_ffn_b1, L0_ffn_W2, L0_ffn_b2):
    import jax
    import jax.numpy as jnp

    def _L0_gnn_ref(x1, x2, G1, G2, eps1, eps2, W1, b1, W2, b2, Wm, bm):
        import jax, jax.numpy as jnp
        import numpy as np
        N = 4096
        D = 128
        L = 3

        def _cxin_conv(x, a, eps, W, b):
            ax = a @ x
            h = ax + (1.0 + eps[0]) * ax
            for i in range(L):
                h = jax.nn.relu(h @ W[i].T + b[i])
            return h
        out1 = _cxin_conv(x1, G1, eps1, W1, b1)
        out2 = _cxin_conv(x2, G2, eps2, W2, b2)
        merged = jnp.concatenate((out1, out2), axis=1)
        return merged @ Wm.T + bm

    def _L0_ffn_ref(x, Wg, bg, W1, b1, W2, b2):
        import jax, jax.numpy as jnp
        import numpy as np
        B, S, D, H, E, K = (8, 4096, 128, 512, 8, 2)
        gate_scores = jnp.einsum('bsd,ed->bse', x, Wg) + bg
        topk_scores, topk_idx = jax.lax.top_k(gate_scores, K)
        topk_probs = jax.nn.softmax(topk_scores, axis=-1)
        combine = jnp.sum(topk_probs[..., None] * jax.nn.one_hot(topk_idx, E, dtype=x.dtype), axis=-2)
        out = jnp.zeros_like(x)
        for e in range(E):
            h = jax.nn.relu(jnp.einsum('bsd,hd->bsh', x, W1[e]) + b1[e])
            y = jnp.einsum('bsh,dh->bsd', h, W2[e]) + b2[e]
            out = out + combine[..., e:e + 1] * y
        return out
    x = x + _L0_gnn_ref(_layernorm(x, axis=-1), L0_gnn_x2, adj, adj, L0_gnn_eps1, L0_gnn_eps2, L0_gnn_W1, L0_gnn_b1, L0_gnn_W2, L0_gnn_b2, L0_gnn_Wm, L0_gnn_bm)
    x = x + _L0_ffn_ref(_layernorm(x, axis=-1)[None], L0_ffn_Wg, L0_ffn_bg, L0_ffn_W1, L0_ffn_b1, L0_ffn_W2, L0_ffn_b2)[0]
    return x

_drawn_inputs = setup_inputs


def setup_inputs(seed=0):
    import zlib

    import numpy as np

    out = dict(_drawn_inputs(seed))
    spreads = {'L0_gnn_b1': (0.0, 0.1), 'L0_gnn_b2': (0.0, 0.1), 'L0_gnn_bm': (0.0, 0.1)}
    factors = {'L0_ffn_b1': 6.278, 'L0_ffn_b2': 5.111}
    for name, (base, spread) in spreads.items():
        noise = np.random.default_rng([zlib.crc32(name.encode()), seed]).standard_normal(out[name].shape)
        drawn = base * np.exp(spread * noise) if base else spread * noise
        out[name] = jnp.asarray(drawn.astype(out[name].dtype))
    for name, factor in factors.items():
        out[name] = (out[name] * factor).astype(out[name].dtype)
    return out
```

```python
from contextlib import ExitStack

import concourse.bass as bass
from concourse import mybir

P = 128
N = 4096
D = 128
NB = 512
BLOCKS = N // NB
KT = N // P
JT = NB // P
E = 8
HID = 512
HC = HID // P
CH = E * HC
LAYERS = 3
EPS = 1e-5

KC = 2
NC = KT // KC
RAW = 4
RING = 4
AHEAD = 3
HR = 3
LAG = 3
WP = 1024
PIECES = 1 + 2 * (CH * P) // WP

F32 = mybir.dt.float32
F32R = mybir.dt.float32r
U32 = mybir.dt.uint32
ALU = mybir.AluOpType
ACT = mybir.ActivationFunctionType

C_EPS, C_CONV_B, C_BM, C_BG, C_B1 = 0, 2, 8, 9, 10
C_ALL = C_B1 + CH

SPLIT_AT = 23
OLD = CH - SPLIT_AT
FIRST_SPLITS = {0: 0, 1: 1, 2: 2}
STEPS_A = (3, 4, 6, 8, 10)
CHAIN = {0: ["h0"], 2: ["layer1"], 4: ["layer2"], 6: ["layer3"], 8: ["merge"],
         OLD + LAG: ["final"], 13: ["rows"], 14: ["norm_a"], 15: ["norm_b"], 17: ["normT"], 19: ["gates"],
         21: ["top_a"], 22: ["top_b"], 24: ["combT"]}
FIRST_B = 25
LAST = FIRST_B + SPLIT_AT


def plan(steps, old, chain, new):
    turns, s, t = [], 0, 0
    last = LAST if new else 0
    middle = [x for x in range(STEPS_A[-1] + 1, FIRST_B)]
    early = len(STEPS_A) + len(middle)
    late = [FIRST_B + (i * SPLIT_AT) // (KT - early) for i in range(KT - early)]
    step_turns = set(STEPS_A) | set(middle) | set(late)
    assert len(step_turns) == KT
    while t < last or (steps and s < KT):
        g = up_old = down_old = up_new = down_new = None
        if old and t < OLD:
            up_old = SPLIT_AT + t
        if old and t < OLD + LAG:
            down_old = SPLIT_AT + t - LAG
        if new and FIRST_B <= t < last:
            up_new = t - FIRST_B
            down_new = up_new - LAG if up_new >= LAG else None
        if steps and s < KT and (t in step_turns or not old):
            g, s = s, s + 1
        stages = [x for x in CHAIN.get(t, []) if (old if x == "final" else chain)]
        split = [g + AHEAD] if g is not None and g + AHEAD < KT else []
        if steps and old and t in FIRST_SPLITS:
            split = [FIRST_SPLITS[t]] + split
        elif steps and new and not old and t == 0:
            split = list(range(AHEAD)) + split
        turns.append((g, split, up_old, down_old, up_new, down_new, stages))
        t += 1
    return turns


def gnn_mixture(nc, adj, x, x2, wsm, w1, w2, wg, b2, small, out):
    with ExitStack() as ctx:
        def sb(name, shape, dt=F32):
            return ctx.enter_context(nc.sbuf_tensor(name, shape, dt))

        def sem(name):
            return ctx.enter_context(nc.semaphore(name))

        Xh = sb("Xh", [P, KT, 2 * D], F32R)
        Xl = sb("Xl", [P, KT, 2 * D], F32R)
        W1h = sb("W1h", [P, CH * P], F32R)
        W1l = sb("W1l", [P, CH * P], F32R)
        W2h = sb("W2h", [P, CH * P], F32R)
        W2l = sb("W2l", [P, CH * P], F32R)
        Wsh = sb("Wsh", [P, WP], F32R)
        Wsl = sb("Wsl", [P, WP], F32R)
        raw = sb("raw", [P, RAW, KC * NB])
        Ah = sb("Ah", [P, RING, NB], F32R)
        Al = sb("Al", [P, RING, NB], F32R)
        hid = sb("hid", [P, 2, NB])
        hidc = sb("hidc", [P, 2, NB])
        Hh = sb("Hh", [P, HR, NB], F32R)
        Hl = sb("Hl", [P, HR, NB], F32R)
        cbS = sb("cbS", [P, 2, NB])
        yo = sb("yo", [P, 2, NB])
        hbuf = sb("hbuf", [P, 2, NB])
        lh = sb("lh", [P, 2, NB], F32R)
        ll = sb("ll", [P, 2, NB], F32R)
        xres = sb("xres", [P, NB])
        b2S, wgS = xres[0:E, 0:D], xres[:, D:D + E]
        xn = sb("xn", [P, NB])
        xTh = sb("xTh", [P, NB], F32R)
        xTl = sb("xTl", [P, NB], F32R)
        cTh = sb("cTh", [E, NB], F32R)
        cTl = sb("cTl", [E, NB], F32R)
        smallS = sb("smallS", [P, C_ALL])
        eps1p = sb("eps1p", [P, 2])
        wgh = sb("wgh", [P, E], F32R)
        wgl = sb("wgl", [P, E], F32R)
        b2h = sb("b2h", [E, D], F32R)
        b2l = sb("b2l", [E, D], F32R)
        ident = sb("ident", [P, P])
        sel = sb("sel", [E, E], F32R)
        iota = sb("iota", [P, JT, E])
        stats = sb("stats", [P, JT, 6])
        mom = sb("mom", [P, 5, JT])
        mean = sb("mean", [P, JT])
        nrm = sb("nrm", [P, 6, JT])
        gS = sb("gS", [P, JT, E])
        top = sb("top", [P, JT, 8])
        topi = sb("topi", [P, JT, 8], U32)
        topf = sb("topf", [P, JT, 2])
        prob = sb("prob", [P, 5, JT])
        comb = sb("comb", [P, 2, JT * E])

        acc = [ctx.enter_context(nc.psum_tensor(f"acc{i}", [P, NB], F32)) for i in range(2)]
        lay = [ctx.enter_context(nc.psum_tensor(f"lay{i}", [P, NB], F32)) for i in range(2)]
        upP = [ctx.enter_context(nc.psum_tensor(f"up{i}", [P, NB], F32)) for i in range(2)]
        yP = ctx.enter_context(nc.psum_tensor("yP", [P, NB], F32))
        misc = ctx.enter_context(nc.psum_tensor("misc", [P, NB], F32))

        def f(ap):
            return ap.bitcast(F32)

        def rows(ap):
            return ap.rearrange("p (j d) -> p j d", j=JT)

        small_in = sem("small_in")
        x_in = [sem(f"x_in{i}") for i in range(2)]
        x2_in = [sem(f"x2_in{i}") for i in range(2)]
        w_in = [sem(f"w_in{i}") for i in range(2)]
        raw_in = [sem(f"raw_in{i}") for i in range(RAW)]
        xres_in, out_dma = sem("xres_in"), sem("out_dma")
        const_step, consts, small_split = sem("const_step"), sem("consts"), sem("small_split")
        x_hi, x_lo, x2_lo, w_hi, w_lo = sem("x_hi"), sem("x_lo"), sem("x2_lo"), sem("w_hi"), sem("w_lo")
        adj_hi, adj_lo, gnn_done, acc_done = sem("adj_hi"), sem("adj_lo"), sem("gnn_done"), sem("acc_done")
        h_hi, h_split, lay_done = sem("h_hi"), sem("h_split"), sem("lay_done")
        merge_psum, merge_sb, merge_rows = sem("merge_psum"), sem("merge_sb"), sem("merge_rows")
        xn_done, ln_step, sd_done = sem("xn_done"), sem("ln_step"), sem("sd_done")
        ln_rstd, ln_done = sem("ln_rstd"), sem("ln_done")
        lnT_psum, xT_hi, xT_lo = sem("lnT_psum"), sem("xT_hi"), sem("xT_lo")
        gates_psum, gates_sb, gates_rows = sem("gates_psum"), sem("gates_sb"), sem("gates_rows")
        top_step, diff_done, exp_done, comb_done = sem("top_step"), sem("diff_done"), sem("exp_done"), sem("comb_done")
        comb_step = sem("comb_step")
        combT_psum, cT_hi, cT_lo = sem("combT_psum"), sem("cT_hi"), sem("cT_lo")
        up_done, relu_done, mult_done = sem("up_done"), sem("relu_done"), sem("mult_done")
        hid_hi, hid_lo, down_done = sem("hid_hi"), sem("hid_lo"), sem("down_done")
        cb_psum, cb_sb = sem("cb_psum"), sem("cb_sb")
        y_sb, y_rows, final_done = sem("y_sb"), sem("y_rows"), sem("final_done")

        LN_STEPS, TOP_STEPS = 8, 6

        def wait(eng, s, value):
            if not isinstance(value, int) or value > 0:
                eng.wait_ge(s, value)

        def before(u):
            if u >= HR:
                return u - HR
            return max(v for v in range(CH) if v % HR == u % HR) - CH

        block = ctx.enter_context(nc.Block())

        @block.sync
        def _(sp):
            def load_x(q):
                if q >= 2:
                    sp.wait_ge(x_lo, q - 1)
                    sp.wait_ge(x2_lo, q - 1)
                sp.dma_start(hid[:, q % 2, :], x[q]).then_inc(x_in[q % 2], 16)
                sp.dma_start(hidc[:, q % 2, :], x2[q]).then_inc(x2_in[q % 2], 16)

            def load_w(i):
                if i >= 2:
                    sp.wait_ge(w_lo, i - 1)
                piece = wsm if i == 0 else (w1, w2)[(i - 1) % 2][(i - 1) // 2]
                sp.dma_start((cbS if i % 2 == 0 else yo)[:, :, :].rearrange("p a n -> p (a n)"),
                             piece).then_inc(w_in[i % 2], 16)

            def load_adj(b, c):
                wait(sp, adj_lo, KT * b + KC * (c - RAW) + KC)
                sp.dma_start(raw[:, c % RAW, :], adj[b, c] if isinstance(b, int) else
                             adj[bass.ds(b, 1), c].rearrange("o p n -> (o p) n")).then_inc(raw_in[c % RAW], 16)

            def row_tile(t, j):
                return t[j] if isinstance(j, int) else t[bass.ds(j, 1)].rearrange("o p n -> (o p) n")

            sp.sem_inc(out_dma, 16)
            load_x(0)
            for c in range(2):
                load_adj(0, c)
            sp.dma_start(smallS[:, :], small).then_inc(small_in, 16)
            sp.dma_start(wgS, wg).then_inc(small_in, 16)
            sp.dma_start(b2S, b2).then_inc(small_in, 16)
            load_x(1)
            for i in range(2):
                load_w(i)
            for c in range(2, NC):
                load_adj(0, c)
                if c % 2 == 0 and 2 + (c - 2) // 2 < BLOCKS:
                    load_x(2 + (c - 2) // 2)
                if c >= 9:
                    load_w(c - 7)

            def body(b):
                for c in range(NC):
                    if not isinstance(b, int) or b < BLOCKS:
                        load_adj(b, c)
                    if c == 1:
                        if isinstance(b, int) and b == 1:
                            sp.wait_ge(small_split, 5)
                        wait(sp, xn_done, b - 1)
                        sp.dma_start(xres[:, :], row_tile(x, b - 1)).then_inc(xres_in, 16)
                    if c == 12 and not (isinstance(b, int) and b < 2):
                        sp.wait_ge(final_done, b - 1)
                        sp.dma_start(row_tile(out, b - 2), yo[:, 1, :]).then_inc(out_dma, 16)

            body(1)
            with sp.Fori(2, BLOCKS) as b:
                body(b)
            body(BLOCKS)
            sp.wait_ge(final_done, BLOCKS)
            sp.dma_start(out[BLOCKS - 1], yo[:, 1, :]).then_inc(out_dma, 16)
            sp.wait_ge(out_dma, 16 * (BLOCKS + 1))

        @block.gpsimd
        def _(pool):
            nc.gpsimd.memset(ident[:, :], 0.0).then_inc(const_step, 1)
            pool.wait_ge(const_step, 1)
            nc.gpsimd.affine_select(out=ident[:, :], in_=ident[:, :], compare_op=ALU.not_equal, fill=1.0, base=0,
                                    pattern=[[-1, P]], channel_multiplier=1).then_inc(consts, 1)
            nc.gpsimd.iota(iota[:, :, :], pattern=[[0, JT], [1, E]], base=0, channel_multiplier=0,
                           allow_small_or_imprecise_dtypes=True).then_inc(consts, 1)

            def x2_low(q):
                pool.wait_ge(x_hi, 2 * q + 2)
                nc.gpsimd.tensor_tensor(Xl[:, JT * q:JT * q + JT, D:2 * D], rows(hidc[:, q % 2, :]),
                                        f(Xh[:, JT * q:JT * q + JT, D:2 * D]), ALU.subtract).then_inc(x2_lo, 1)

            def w_low(i):
                pool.wait_ge(w_hi, i + 1)
                src = (cbS if i % 2 == 0 else yo)[:, :, :].rearrange("p a n -> p (a n)")
                if i == 0:
                    hi, lo = Wsh[:, :], Wsl[:, :]
                else:
                    at = slice(WP * ((i - 1) // 2), WP * ((i - 1) // 2 + 1))
                    hi, lo = ((W1h, W1l) if i % 2 else (W2h, W2l))
                    hi, lo = hi[:, at], lo[:, at]
                nc.gpsimd.tensor_tensor(lo, src, f(hi), ALU.subtract).then_inc(w_lo, 1)

            x2_low(0)
            for s in range(KT):
                if s % 4 == 0 and s // 4 + 1 < BLOCKS:
                    x2_low(s // 4 + 1)
                if s >= 12 and s % 2 == 0 and (s - 12) // 2 < PIECES:
                    w_low((s - 12) // 2)

        @block.tensor
        def _(pe):
            def three(ps, wh, wl, ih, il, start, stop):
                pe.matmul(ps, wh, ih, start=start, stop=False)
                pe.matmul(ps, wh, il, start=False, stop=False)
                return pe.matmul(ps, wl, ih, start=False, stop=stop)

            def gnn(b, s):
                if isinstance(b, int) and b == 0 and s % 4 == 0:
                    pe.wait_ge(x_lo, s // 4 + 1)
                    pe.wait_ge(x2_lo, s // 4 + 1)
                pe.wait_ge(adj_lo, KT * b + s + 1)
                for half in range(2):
                    if s == 0:
                        wait(pe, h_split, 8 * (b - 1) + half + 1)
                    at = slice(half * D, half * D + D)
                    last = three(acc[half][:, :], Xh[:, s, at], Xl[:, s, at], Ah[:, s % RING, :],
                                 Al[:, s % RING, :], s == 0, s == KT - 1)
                    if s == KT - 1:
                        last.then_inc(acc_done, 1)
                if s < KT - 1:
                    last.then_inc(gnn_done, 1)
                else:
                    pe.wait_ge(acc_done, 2 * b + 2)
                    pe.sem_inc(gnn_done, 1)

            def up(j, u):
                if u == 0:
                    pe.wait_ge(xT_lo, j + 1)
                wait(pe, relu_done, CH * j + u - 1)
                at = slice(u * P, u * P + P)
                three(upP[u % 2][:, :], W1h[:, at], W1l[:, at], xTh[:, :], xTl[:, :], True, True)\
                    .then_inc(up_done, 1)
                if u == 0:
                    spread(j, 0)
                    wait(pe, y_sb, j)
                    three(yP[:, :], b2h[:, :], b2l[:, :], cTh[:, :], cTl[:, :], True, False)
                if u % HC == 2 and u // HC + 1 < E:
                    spread(j, u // HC + 1)

            def spread(j, e):
                if e == 0:
                    pe.wait_ge(cT_lo, j + 1)
                    wait(pe, final_done, j)
                wait(pe, cb_sb, E * j + e)
                pe.matmul(misc[:, :], sel[:, e:e + 1].to_broadcast([E, P]), cTh[:, :], start=True, stop=False)
                pe.matmul(misc[:, :], sel[:, e:e + 1].to_broadcast([E, P]), cTl[:, :], start=False, stop=True).then_inc(cb_psum, 1)

            def down(j, u):
                pe.wait_ge(hid_lo, CH * j + u + 1)
                at = slice(u * P, u * P + P)
                three(yP[:, :], W2h[:, at], W2l[:, at], Hh[:, u % HR, :], Hl[:, u % HR, :], False, u == CH - 1)\
                    .then_inc(down_done, 1)

            def turn_rows(dst, src):
                for t in range(JT):
                    at = slice(t * P, t * P + P)
                    last = pe.transpose(dst[:, at], src[:, at], ident[:, :])
                return last

            def stage(name, j):
                if name.startswith("layer"):
                    l = int(name[5:])
                    for half in range(2):
                        pe.wait_ge(h_split, 8 * j + 2 * (l - 1) + half + 1)
                        at = slice((half * LAYERS + l - 1) * D, (half * LAYERS + l) * D)
                        three(lay[half][:, :], Wsh[:, at], Wsl[:, at], lh[:, half, :], ll[:, half, :], True, True)\
                            .then_inc(lay_done, 1)
                elif name == "merge":
                    for half in range(2):
                        pe.wait_ge(h_split, 8 * j + 6 + half + 1)
                        at = slice((2 * LAYERS + half) * D, (2 * LAYERS + half + 1) * D)
                        last = three(lay[0][:, :], Wsh[:, at], Wsl[:, at], lh[:, half, :], ll[:, half, :],
                                     half == 0, half == 1)
                    last.then_inc(merge_psum, 1)
                elif name == "rows":
                    pe.wait_ge(merge_sb, j + 1)
                    turn_rows(lay[1], hbuf[:, 0, :]).then_inc(merge_rows, 1)
                elif name == "normT":
                    pe.wait_ge(ln_done, BLOCKS + j + 1)
                    turn_rows(lay[0], hbuf[:, 0, :]).then_inc(lnT_psum, 1)
                elif name == "gates":
                    pe.wait_ge(xT_lo, j + 1)
                    three(lay[1][0:E, :], wgh[:, :], wgl[:, :], xTh[:, :], xTl[:, :], True, True)\
                        .then_inc(gates_psum, 1)
                elif name == "top_a":
                    pe.wait_ge(gates_sb, j + 1)
                    for t in range(JT):
                        last = pe.matmul(lay[0][:, t * E:t * E + E], hbuf[0:E, 1, t * P:t * P + P],
                                         ident[0:E, 0:E], start=True, stop=True)
                    last.then_inc(gates_rows, 1)
                elif name == "combT":
                    pe.wait_ge(comb_done, j + 1)
                    for t in range(JT):
                        last = pe.matmul(lay[1][0:E, t * P:t * P + P], comb[:, 0, t * E:t * E + E],
                                         ident[:, :], start=True, stop=True)
                    last.then_inc(combT_psum, 1)

            def final(j):
                pe.wait_ge(y_sb, j + 1)
                turn_rows(misc, yo[:, 0, :]).then_inc(y_rows, 1)

            def body(b, turns):
                for g, split, up_old, down_old, up_new, down_new, stages in turns:
                    for name in stages:
                        if name == "final":
                            final(b - 2)
                        elif name != "h0":
                            stage(name, b - 1)
                    if up_old is not None:
                        up(b - 2, up_old)
                    if up_new is not None:
                        up(b - 1, up_new)
                    if g is not None:
                        gnn(b, g)
                    if down_old is not None:
                        down(b - 2, down_old)
                    if down_new is not None:
                        down(b - 1, down_new)

            pe.wait_ge(consts, 3)
            body(0, plan(True, False, False, False))
            pe.wait_ge(w_lo, PIECES)
            pe.wait_ge(small_split, 5)
            body(1, plan(True, False, True, True))
            with pe.Fori(2, BLOCKS) as b:
                body(b, plan(True, True, True, True))
            body(BLOCKS, plan(False, True, True, True))
            for u in range(SPLIT_AT, CH + LAG):
                if u < CH:
                    up(BLOCKS - 1, u)
                down(BLOCKS - 1, u - LAG)
            final(BLOCKS - 1)

        @block.scalar
        def _(act):
            def high(dst, src):
                return nc.scalar.activation(dst, src, ACT.Copy)

            def adj_high(b, k):
                c, slot = k // KC, (k // KC) % RAW
                act.wait_ge(raw_in[slot], 16 * (NC // RAW * b + c // RAW + 1))
                wait(act, gnn_done, KT * b + k - RING + 1)
                high(Ah[:, k % RING, :], raw[:, slot, (k % KC) * NB:(k % KC + 1) * NB]).then_inc(adj_hi, 1)

            def x_high(q):
                at = slice(JT * q, JT * q + JT)
                act.wait_ge(x2_in[q % 2], 16 * (q // 2 + 1))
                high(Xh[:, at, D:2 * D], rows(hidc[:, q % 2, :])).then_inc(x_hi, 1)
                act.wait_ge(ln_step, LN_STEPS * q + 4)
                act.activation(nrm[:, 1, :], nrm[:, 0, :], ACT.Sqrt).then_inc(sd_done, 1)
                act.wait_ge(ln_done, q + 1)
                high(Xh[:, at, 0:D], rows(hid[:, q % 2, :])).then_inc(x_hi, 1)

            def w_high(i):
                act.wait_ge(w_in[i % 2], 16 * (i // 2 + 1))
                src = (cbS if i % 2 == 0 else yo)[:, :, :].rearrange("p a n -> p (a n)")
                at = slice(WP * ((i - 1) // 2), WP * ((i - 1) // 2 + 1))
                dst = Wsh[:, :] if i == 0 else (W1h if i % 2 else W2h)[:, at]
                high(dst, src).then_inc(w_hi, 1)

            def relu(j, u):
                act.wait_ge(up_done, CH * j + u + 1)
                wait(act, mult_done, CH * j + u - 1)
                nc.scalar.activation(hid[:, u % 2, :], upP[u % 2][:, :], ACT.Relu,
                                     bias=smallS[:, C_B1 + u:C_B1 + u + 1]).then_inc(relu_done, 1)
                if u == 0:
                    spread(j, 0)
                if u % HC == 2 and u // HC + 1 < E:
                    spread(j, u // HC + 1)

            def spread(j, e):
                act.wait_ge(cb_psum, E * j + e + 1)
                wait(act, mult_done, CH * j + HC * (e - 1))
                nc.scalar.activation(cbS[:, e % 2, :], misc[:, :], ACT.Copy).then_inc(cb_sb, 1)

            def hid_high(j, u):
                act.wait_ge(mult_done, CH * j + u + 1)
                wait(act, down_done, CH * j + before(u) + 1)
                high(Hh[:, u % HR, :], hidc[:, u % 2, :]).then_inc(hid_hi, 1)

            def stage(name, j):
                if name == "h0":
                    wait(act, merge_psum, j)
                    for half in range(2):
                        act.wait_ge(acc_done, 2 * j + half + 1)
                        nc.scalar.activation(lh[:, half, :], acc[half][:, :], ACT.Copy,
                                             scale=eps1p[:, half:half + 1]).then_inc(h_hi, 1)
                elif name.startswith("layer"):
                    l = int(name[5:])
                    for half in range(2):
                        act.wait_ge(lay_done, 6 * j + 2 * (l - 1) + half + 1)
                        bias = smallS[:, C_CONV_B + half * LAYERS + l - 1:C_CONV_B + half * LAYERS + l]
                        nc.scalar.activation(hbuf[:, half, :], lay[half][:, :], ACT.Relu, bias=bias)
                        nc.scalar.activation(lh[:, half, :], lay[half][:, :], ACT.Relu, bias=bias)\
                            .then_inc(h_hi, 1)
                elif name == "merge":
                    act.wait_ge(merge_psum, j + 1)
                    nc.scalar.activation(hbuf[:, 0, :], lay[0][:, :], ACT.Identity,
                                         bias=smallS[:, C_BM:C_BM + 1]).then_inc(merge_sb, 1)
                elif name == "norm_b":
                    act.wait_ge(ln_step, LN_STEPS * (BLOCKS + j) + 4)
                    act.activation(nrm[:, 1, :], nrm[:, 0, :], ACT.Sqrt).then_inc(sd_done, 1)
                elif name == "normT":
                    act.wait_ge(lnT_psum, j + 1)
                    wait(act, up_done, CH * j)
                    high(xTh[:, :], lay[0][:, :]).then_inc(xT_hi, 1)
                elif name == "gates":
                    act.wait_ge(gates_psum, j + 1)
                    nc.scalar.activation(hbuf[0:E, 1, :], lay[1][0:E, :], ACT.Identity,
                                         bias=smallS[0:E, C_BG:C_BG + 1]).then_inc(gates_sb, 1)
                elif name == "top_b":
                    act.wait_ge(diff_done, j + 1)
                    nc.scalar.activation(prob[:, 1, :], prob[:, 0, :], ACT.Exp).then_inc(exp_done, 1)
                elif name == "combT":
                    act.wait_ge(combT_psum, j + 1)
                    wait(act, cb_psum, E * j)
                    high(cTh[:, :], lay[1][0:E, :]).then_inc(cT_hi, 1)

            def final(j):
                act.wait_ge(down_done, CH * j + CH)
                nc.scalar.activation(yo[:, 0, :], yP[:, :], ACT.Copy).then_inc(y_sb, 1)

            def body(b, turns):
                first = isinstance(b, int) and b == 0
                for g, split, up_old, down_old, up_new, down_new, stages in turns:
                    for name in stages:
                        if name == "final":
                            final(b - 2)
                        else:
                            stage(name, b - 1)
                    if up_old is not None:
                        relu(b - 2, up_old)
                        hid_high(b - 2, up_old - 1)
                    elif down_old == CH - LAG:
                        hid_high(b - 2, CH - 1)
                    if up_new is not None:
                        relu(b - 1, up_new)
                        if up_new > 0:
                            hid_high(b - 1, up_new - 1)
                    for k in split:
                        adj_high(b, k)
                    if first:
                        if g % 4 == 0 and g // 4 + 1 < BLOCKS:
                            x_high(g // 4 + 1)
                        if g >= 12 and g % 2 == 0 and (g - 12) // 2 < PIECES:
                            w_high((g - 12) // 2)

            for k in range(AHEAD - 1):
                adj_high(0, k)
            x_high(0)
            adj_high(0, AHEAD - 1)
            act.wait_ge(small_in, 48)
            high(wgh[:, :], wgS).then_inc(small_split, 1)
            high(b2h[:, :], b2S).then_inc(small_split, 1)
            act.wait_ge(consts, 2)
            high(sel[:, :], ident[0:E, 0:E]).then_inc(consts, 1)
            body(0, plan(True, False, False, False))
            body(1, plan(True, False, True, True))
            with act.Fori(2, BLOCKS) as b:
                body(b, plan(True, True, True, True))
            body(BLOCKS, plan(False, True, True, True))
            for u in range(SPLIT_AT, CH + 1):
                if u < CH:
                    relu(BLOCKS - 1, u)
                hid_high(BLOCKS - 1, u - 1)
            final(BLOCKS - 1)

        @block.vector
        def _(dve):
            def low(dst, src, hi):
                return nc.vector.tensor_tensor(dst, src, f(hi), ALU.subtract)

            def adj_low(b, k):
                dve.wait_ge(adj_hi, KT * b + k + 1)
                low(Al[:, k % RING, :], raw[:, (k // KC) % RAW, (k % KC) * NB:(k % KC + 1) * NB],
                    Ah[:, k % RING, :]).then_inc(adj_lo, 1)

            def variance(use, src):
                base = LN_STEPS * use
                for t in range(JT):
                    last = nc.vector.bn_stats(stats[:, t, :], src[:, t * D:t * D + D])
                last.then_inc(ln_step, 1)
                dve.wait_ge(ln_step, base + 1)
                nc.vector.tensor_tensor(mom[:, 0, :], stats[:, :, 1], stats[:, :, 4], ALU.add)
                nc.vector.tensor_tensor(mom[:, 1, :], stats[:, :, 1], stats[:, :, 4], ALU.subtract)
                nc.vector.tensor_tensor(mom[:, 2, :], stats[:, :, 2], stats[:, :, 5], ALU.add).then_inc(ln_step, 1)
                dve.wait_ge(ln_step, base + 2)
                nc.vector.tensor_scalar(mean[:, :], mom[:, 0, :], 0.5, None, ALU.mult)
                nc.vector.tensor_tensor(mom[:, 3, :], mom[:, 1, :], mom[:, 1, :], ALU.mult)
                nc.vector.tensor_scalar(mom[:, 4, :], mom[:, 2, :], 1.0 / D, EPS, ALU.mult, ALU.add)\
                    .then_inc(ln_step, 1)
                dve.wait_ge(ln_step, base + 3)
                nc.vector.scalar_tensor_tensor(out=nrm[:, 0, :], in0=mom[:, 3, :], scalar=0.25, in1=mom[:, 4, :],
                                               op0=ALU.mult, op1=ALU.add).then_inc(ln_step, 1)

            def normalise(use, dst, src):
                base = LN_STEPS * use
                dve.wait_ge(sd_done, use + 1)
                nc.vector.reciprocal(nrm[:, 2, :], nrm[:, 1, :]).then_inc(ln_step, 1)
                dve.wait_ge(ln_step, base + 5)
                nc.vector.tensor_tensor(nrm[:, 3, :], nrm[:, 2, :], nrm[:, 2, :], ALU.mult).then_inc(ln_step, 1)
                dve.wait_ge(ln_step, base + 6)
                nc.vector.tensor_tensor(nrm[:, 4, :], nrm[:, 3, :], nrm[:, 0, :], ALU.mult).then_inc(ln_step, 1)
                dve.wait_ge(ln_step, base + 7)
                nc.vector.tensor_scalar(nrm[:, 3, :], nrm[:, 4, :], -0.5, 1.5, ALU.mult, ALU.add).then_inc(ln_step, 1)
                dve.wait_ge(ln_step, base + 8)
                nc.vector.tensor_tensor(nrm[:, 5, :], nrm[:, 3, :], nrm[:, 2, :], ALU.mult).then_inc(ln_rstd, 1)
                dve.wait_ge(ln_rstd, use + 1)
                for t in range(JT):
                    at = slice(t * D, t * D + D)
                    last = nc.vector.tensor_scalar(dst[:, at], src[:, at], mean[:, t:t + 1], nrm[:, 5, t:t + 1],
                                                   ALU.subtract, ALU.mult)
                last.then_inc(ln_done, 1)

            def x_prepare(q):
                at = slice(JT * q, JT * q + JT)
                dve.wait_ge(x_in[q % 2], 16 * (q // 2 + 1))
                variance(q, hid[:, q % 2, :])
                normalise(q, hid[:, q % 2, :], hid[:, q % 2, :])
                dve.wait_ge(x_hi, 2 * q + 2)
                low(Xl[:, at, 0:D], rows(hid[:, q % 2, :]), Xh[:, at, 0:D]).then_inc(x_lo, 1)

            def mult(j, u):
                wait(dve, hid_lo, CH * j + u - 1)
                dve.wait_ge(relu_done, CH * j + u + 1)
                if u % HC == 0:
                    dve.wait_ge(cb_sb, E * j + u // HC + 1)
                nc.vector.tensor_tensor(hidc[:, u % 2, :], hid[:, u % 2, :], cbS[:, (u // HC) % 2, :],
                                        ALU.mult).then_inc(mult_done, 1)

            def hid_low(j, u):
                dve.wait_ge(hid_hi, CH * j + u + 1)
                low(Hl[:, u % HR, :], hidc[:, u % 2, :], Hh[:, u % HR, :]).then_inc(hid_lo, 1)

            def stage(name, j):
                if name == "h0":
                    for half in range(2):
                        dve.wait_ge(h_hi, 8 * j + half + 1)
                        nc.vector.scalar_tensor_tensor(out=ll[:, half, :], in0=acc[half][:, :],
                                                       scalar=eps1p[:, half:half + 1], in1=f(lh[:, half, :]),
                                                       op0=ALU.mult, op1=ALU.subtract).then_inc(h_split, 1)
                elif name.startswith("layer"):
                    l = int(name[5:])
                    for half in range(2):
                        dve.wait_ge(h_hi, 8 * j + 2 * l + half + 1)
                        low(ll[:, half, :], hbuf[:, half, :], lh[:, half, :]).then_inc(h_split, 1)
                elif name == "rows":
                    dve.wait_ge(merge_rows, j + 1)
                    wait(dve, final_done, j)
                    dve.wait_ge(xres_in, 16 * j + 16)
                    nc.vector.tensor_tensor(xn[:, :], lay[1][:, :], xres[:, :], ALU.add).then_inc(xn_done, 1)
                elif name == "norm_a":
                    dve.wait_ge(xn_done, j + 1)
                    variance(BLOCKS + j, xn)
                elif name == "norm_b":
                    normalise(BLOCKS + j, hbuf[:, 0, :], xn)
                elif name == "normT":
                    dve.wait_ge(xT_hi, j + 1)
                    low(xTl[:, :], lay[0][:, :], xTh[:, :]).then_inc(xT_lo, 1)
                elif name == "top_a":
                    base = TOP_STEPS * j
                    dve.wait_ge(gates_rows, j + 1)
                    scores = lay[0][:, 0:JT * E].rearrange("p (j e) -> p j e", j=JT)
                    nc.vector.tensor_copy(gS[:, :, :], scores)
                    for t in range(JT):
                        last = nc.vector.max(top[:, t, :], scores[:, t, :])
                    last.then_inc(top_step, 1)
                    dve.wait_ge(top_step, base + 1)
                    nc.vector.tensor_tensor(prob[:, 0, :], top[:, :, 1], top[:, :, 0], ALU.subtract)\
                        .then_inc(diff_done, 1)
                    for t in range(JT):
                        last = nc.vector.max_index(topi[:, t, :], top[:, t, :], gS[:, t, :])
                    last.then_inc(top_step, 1)
                    dve.wait_ge(top_step, base + 2)
                    nc.vector.tensor_copy(topf[:, :, :], topi[:, :, 0:2]).then_inc(top_step, 1)
                elif name == "top_b":
                    base = TOP_STEPS * j
                    wide = [P, JT, E]
                    dve.wait_ge(exp_done, j + 1)
                    nc.vector.tensor_scalar(prob[:, 2, :], prob[:, 1, :], 1.0, None, ALU.add).then_inc(top_step, 1)
                    dve.wait_ge(top_step, base + 4)
                    nc.vector.reciprocal(prob[:, 3, :], prob[:, 2, :]).then_inc(top_step, 1)
                    dve.wait_ge(top_step, base + 5)
                    nc.vector.tensor_tensor(prob[:, 4, :], prob[:, 1, :], prob[:, 3, :], ALU.mult)
                    for i in range(2):
                        last = nc.vector.tensor_tensor(
                            rows_e(comb[:, i, :]), iota[:, :, :],
                            topf[:, :, i:i + 1].to_broadcast(wide), ALU.is_equal)
                    last.then_inc(top_step, 1)
                    dve.wait_ge(top_step, base + 6)
                    for i in range(2):
                        last = nc.vector.tensor_tensor(
                            rows_e(comb[:, i, :]), rows_e(comb[:, i, :]),
                            prob[:, 3 + i, :].rearrange("p (j o) -> p j o", o=1).to_broadcast(wide), ALU.mult)
                    last.then_inc(comb_step, 1)
                    dve.wait_ge(comb_step, j + 1)
                    nc.vector.tensor_tensor(comb[:, 0, :], comb[:, 0, :], comb[:, 1, :], ALU.add)\
                        .then_inc(comb_done, 1)
                elif name == "combT":
                    dve.wait_ge(cT_hi, j + 1)
                    low(cTl[:, :], lay[1][0:E, :], cTh[:, :]).then_inc(cT_lo, 1)

            def rows_e(ap):
                return ap.rearrange("p (j e) -> p j e", j=JT)

            def final(j):
                dve.wait_ge(y_rows, j + 1)
                dve.wait_ge(out_dma, 16 * j + 16)
                nc.vector.tensor_tensor(yo[:, 1, :], misc[:, :], xn[:, :], ALU.add).then_inc(final_done, 1)

            def body(b, turns):
                first = isinstance(b, int) and b == 0
                for g, split, up_old, down_old, up_new, down_new, stages in turns:
                    for name in stages:
                        if name == "final":
                            final(b - 2)
                        else:
                            stage(name, b - 1)
                    if up_old is not None:
                        mult(b - 2, up_old)
                        hid_low(b - 2, up_old - 1)
                    elif down_old == CH - LAG:
                        hid_low(b - 2, CH - 1)
                    if up_new is not None:
                        mult(b - 1, up_new)
                        if up_new > 0:
                            hid_low(b - 1, up_new - 1)
                    for k in split:
                        adj_low(b, k)
                    if first and g % 4 == 0 and g // 4 + 1 < BLOCKS:
                        x_prepare(g // 4 + 1)

            for k in range(AHEAD - 1):
                adj_low(0, k)
            x_prepare(0)
            adj_low(0, AHEAD - 1)
            dve.wait_ge(small_in, 48)
            dve.wait_ge(small_split, 2)
            low(wgl[:, :], wgS, wgh[:, :]).then_inc(small_split, 1)
            low(b2l[:, :], b2S, b2h[:, :]).then_inc(small_split, 1)
            nc.vector.tensor_scalar(eps1p[:, :], smallS[:, C_EPS:C_EPS + 2], 1.0, 1.0, ALU.add, ALU.add)\
                .then_inc(small_split, 1)
            dve.wait_ge(consts, 2)
            body(0, plan(True, False, False, False))
            body(1, plan(True, False, True, True))
            with dve.Fori(2, BLOCKS) as b:
                body(b, plan(True, True, True, True))
            body(BLOCKS, plan(False, True, True, True))
            for u in range(SPLIT_AT, CH + 1):
                if u < CH:
                    mult(BLOCKS - 1, u)
                hid_low(BLOCKS - 1, u - 1)
            final(BLOCKS - 1)


def kernel(x, adj, L0_gnn_x2, L0_gnn_eps1, L0_gnn_eps2, L0_gnn_W1, L0_gnn_b1, L0_gnn_W2, L0_gnn_b2, L0_gnn_Wm,
           L0_gnn_bm, L0_ffn_Wg, L0_ffn_bg, L0_ffn_W1, L0_ffn_b1, L0_ffn_W2, L0_ffn_b2):
    import numpy as np
    import concourse.bacc as bacc
    from concourse.bass_utils import run_bass_kernel_spmd

    def row_blocks(a):
        return np.ascontiguousarray(np.asarray(a).reshape(BLOCKS, JT, P, D).transpose(0, 2, 1, 3)).reshape(BLOCKS, P, NB)

    adj_l = np.asarray(adj).reshape(BLOCKS, NB, NC, KC, P).transpose(0, 2, 4, 3, 1)
    adj_l = np.ascontiguousarray(adj_l).reshape(BLOCKS, NC, P, KC * NB)
    wm = np.asarray(L0_gnn_Wm)
    wsm = np.concatenate([np.asarray(w)[i].T for w in (L0_gnn_W1, L0_gnn_W2) for i in range(LAYERS)]
                         + [wm[:, 0:D].T, wm[:, D:2 * D].T], axis=1)
    w1 = np.asarray(L0_ffn_W1).transpose(2, 0, 1).reshape(D, CH * P)
    w2 = np.asarray(L0_ffn_W2).reshape(E, D, HC, P).transpose(3, 0, 2, 1).reshape(P, CH * D)

    def pieces(w):
        return np.ascontiguousarray(w.reshape(P, -1, WP).transpose(1, 0, 2))

    small = np.zeros((P, C_ALL), np.float32)
    small[:, C_EPS] = np.asarray(L0_gnn_eps1)[0]
    small[:, C_EPS + 1] = np.asarray(L0_gnn_eps2)[0]
    small[:, C_CONV_B:C_CONV_B + LAYERS] = np.asarray(L0_gnn_b1).T
    small[:, C_CONV_B + LAYERS:C_CONV_B + 2 * LAYERS] = np.asarray(L0_gnn_b2).T
    small[:, C_BM] = np.asarray(L0_gnn_bm)
    small[0:E, C_BG] = np.asarray(L0_ffn_bg)
    small[:, C_B1:C_ALL] = np.asarray(L0_ffn_b1).reshape(CH, P).T
    arrays = {
        "adj_l": adj_l, "x_rows": row_blocks(x), "x2_rows": row_blocks(L0_gnn_x2),
        "wsm": np.ascontiguousarray(wsm), "w1": pieces(w1), "w2": pieces(w2),
        "wg": np.ascontiguousarray(np.asarray(L0_ffn_Wg).T), "b2": np.ascontiguousarray(L0_ffn_b2), "small": small,
    }
    nc = bacc.Bacc("TRN2", target_bir_lowering=False, num_devices=1, dynamic_dma_scratch_size=512)
    args = [nc.dram_tensor(n, a.shape, F32, kind="ExternalInput").ap() for n, a in arrays.items()]
    out = nc.dram_tensor("out_rows", (BLOCKS, P, NB), F32, kind="ExternalOutput").ap()
    gnn_mixture(nc, *args, out)
    r = run_bass_kernel_spmd(nc, [arrays], core_ids=[0])
    got = np.asarray(r.results[0]["out_rows"])
    return got.reshape(BLOCKS, P, JT, D).transpose(0, 2, 1, 3).reshape(N, D)
```

```python
from contextlib import ExitStack

import concourse.bass as bass
from concourse import mybir

P = 128
N = 4096
D = 128
NB = 512
BLOCKS = N // NB
KT = N // P
JT = NB // P
E = 8
TOP = 2
HID = 512
HC = HID // P
LAYERS = 3
EPS = 1e-5

KC = 2
NC = KT // KC
RAW = 4
RING = 4
AHEAD = 3

TS = 256
TA = TS // P
GROUP_BLOCKS = (6, 2)
CAP = tuple(n * NB for n in GROUP_BLOCKS)
STRIDE = tuple(c + TS for c in CAP)
TILES = tuple((TOP * c // TS + E - 1 + 1) // 2 * 2 for c in CAP)
FIRST_TILE = (0, TILES[0])
ALL_TILES = sum(TILES)
WR = 4
WS = 4 * HID

F32 = mybir.dt.float32
F32R = mybir.dt.float32r
U32 = mybir.dt.uint32
I32 = mybir.dt.int32
ALU = mybir.AluOpType
ACT = mybir.ActivationFunctionType
AX = mybir.AxisListType

C_EPS, C_CONV_B, C_BM, C_BG = 0, 2, 8, 9
C_ALL = 10

CHAIN = {0: ["h0"], 2: ["layer1"], 5: ["layer2"], 8: ["layer3"], 11: ["merge"], 13: ["rows"], 14: ["norm_a"],
         15: ["norm_b"], 17: ["normT"], 19: ["gates"], 21: ["top_a"], 22: ["top_b"], 24: ["rank"], 26: ["close"]}
LAST_CHAIN = {0: ["h0"], 1: ["layer1"], 2: ["layer2"], 3: ["layer3"], 4: ["merge"], 5: ["rows"], 6: ["norm_a", "norm_b"],
              7: ["normT"], 8: ["gates"], 9: ["top_a"], 10: ["top_b"], 11: ["rank"], 12: ["close"]}
IN_BODY_7 = 15
SPLIT_W = {0: {12: 0, 20: 1, 28: 2}, 1: {4 * i: 3 + i for i in range(E - 2)}}


def plan(b):
    if b == BLOCKS:
        return [(None, [], LAST_CHAIN.get(t, []), IN_BODY_7 + t) for t in range(TILES[0] - IN_BODY_7)]
    turns = []
    for t in range(KT):
        split = [t + AHEAD] if t + AHEAD < KT or b < BLOCKS - 1 else []
        stages = [x for x in CHAIN.get(t, []) if b > 0 and (x != "close" or b == GROUP_BLOCKS[0])]
        before, after = t * IN_BODY_7 // KT, (t + 1) * IN_BODY_7 // KT
        turns.append((t, split, stages, before if b == BLOCKS - 1 and after > before else None))
    return turns


def gnn_mixture(nc, adj, x, x2, wsm, wraw, wg, small, bset, out, wset, keepd, xs, ys):
    with ExitStack() as ctx:
        def sb(name, shape, dt=F32):
            return ctx.enter_context(nc.sbuf_tensor(name, shape, dt))

        def sem(name):
            return ctx.enter_context(nc.semaphore(name))

        Xh = sb("Xh", [P, KT, 2 * D], F32R)
        Xl = sb("Xl", [P, KT, 2 * D], F32R)
        Wsh = sb("Wsh", [P, 2 * HID], F32R)
        Wsl = sb("Wsl", [P, 2 * HID], F32R)
        raw = sb("raw", [P, RAW, KC * NB])
        Ah = sb("Ah", [P, RING, NB], F32R)
        Al = sb("Al", [P, RING, NB], F32R)
        hbuf = sb("hbuf", [P, 2, NB])
        lh = sb("lh", [P, 2, NB], F32R)
        ll = sb("ll", [P, 2, NB], F32R)
        lnr = sb("lnr", [P, NB])
        KEEP = NB + 2 * TOP * JT
        keep = sb("keep", [P, KEEP])
        xres = sb("xres", [P, NB])
        xTh = sb("xTh", [P, NB], F32R)
        xTl = sb("xTl", [P, NB], F32R)
        wbuf = sb("wbuf", [P, WR, WS], F32R)
        bbuf = sb("bbuf", [P, WR, 8])
        xr = sb("xr", [P, WR, TS])
        tTh = sb("tTh", [P, 2, TS], F32R)
        tTl = sb("tTl", [P, 2, TS], F32R)
        th = sb("th", [P, 2, NB])
        tHh = sb("tHh", [P, 2, 2, NB], F32R)
        tHl = sb("tHl", [P, 2, 2, NB], F32R)
        tyT = sb("tyT", [P, 2, TS])
        tyr = sb("tyr", [P, 2, TS])
        rawx2 = sb("rawx2", [P, 2, NB])
        stage_w = sb("stage_w", [P, 2, 2 * HID])
        keepS = sb("keepS", [P, 2, KEEP])
        smallS = sb("smallS", [P, C_ALL])
        eps1p = sb("eps1p", [P, 2])
        wgS = sb("wgS", [P, E])
        wgh = sb("wgh", [P, E], F32R)
        wgl = sb("wgl", [P, E], F32R)
        zero = sb("zero", [P, P])
        ident = sb("ident", [P, P])
        ones = sb("ones", [P, P])
        earlier = sb("earlier", [P, P])
        iota = sb("iota", [P, JT, E])
        stats = sb("stats", [P, JT, 6])
        mom = sb("mom", [P, 5, JT])
        mean = sb("mean", [P, JT])
        nrm = sb("nrm", [P, 6, JT])
        gS = sb("gS", [P, JT, E])
        top = sb("top", [P, JT, 8])
        topi = sb("topi", [P, JT, 8], U32)
        topf = sb("topf", [P, JT, TOP])
        prob = sb("prob", [P, 3, JT])
        chose = sb("chose", [P, TOP, JT * E])
        chosen = sb("chosen", [P, (JT + 1) * E])
        bases = [sb(f"base{g}", [P, E]) for g in range(2)]
        nextslot = sb("nextslot", [P, E])
        place = sb("place", [P, JT, E])
        picked = sb("picked", [P, TOP, JT * E])
        slots = sb("slots", [P, TOP * JT], U32)
        MT = CAP[0] // TS
        steps_of = sb("steps_of", [P, E, MT])
        upto = sb("upto", [P, E, E])
        count = sb("count", [P, 4, E])
        wide8 = sb("wide8", [P, E, E])
        wideM = sb("wideM", [P, E, MT])
        tilei = sb("tilei", [1, TILES[0]])
        passed = sb("passed", [1, 2, TILES[0] * E])
        tt = sb("tt", [1, 7, TILES[0]])
        tab = [sb(f"tab{g}", [1, 2, TILES[g]], I32) for g in range(2)]
        ends_at = [sb(f"ends_at{g}", [1, E], I32) for g in range(2)]
        moved = [sb(f"moved{g}", [P, E]) for g in range(2)]
        beyond = sb("beyond", [P, 2, TOP * JT * E])
        rowf = sb("rowf", [P, TOP * JT])
        resrow = sb("resrow", [P, 2, TOP * JT], U32)

        gathered = stage_w[:, :, :].rearrange("p a (i d) -> p a i d", d=D)

        acc = [ctx.enter_context(nc.psum_tensor(f"acc{i}", [P, NB], F32)) for i in range(2)]
        lay = [ctx.enter_context(nc.psum_tensor(f"lay{i}", [P, NB], F32)) for i in range(2)]
        upP = [ctx.enter_context(nc.psum_tensor(f"up{i}", [P, NB], F32)) for i in range(2)]
        tin = ctx.enter_context(nc.psum_tensor("tin", [P, NB], F32))
        ty = ctx.enter_context(nc.psum_tensor("ty", [P, NB], F32))

        def f(ap):
            return ap.bitcast(F32)

        def rows(ap):
            return ap.rearrange("p (j d) -> p j d", j=JT)

        def by_expert(ap):
            return ap.rearrange("p (j e) -> p j e", e=E)

        keep_p = keep[:, NB:NB + TOP * JT].rearrange("p (i j) -> p i j", i=TOP)
        keep_slot = keep[:, NB + TOP * JT:KEEP]

        sums = [upP, acc]

        small_in = sem("small_in")
        x_in = [sem(f"x_in{i}") for i in range(2)]
        x2_in = [sem(f"x2_in{i}") for i in range(2)]
        w_in = [sem(f"w_in{i}") for i in range(2)]
        raw_in = [sem(f"raw_in{i}") for i in range(RAW)]
        xres_in, wset_out, zero_out, keep_out = sem("xres_in"), sem("wset_out"), sem("zero_out"), sem("keep_out")
        ends_known = sem("ends_known")
        const_step, consts, small_split = sem("const_step"), sem("consts"), sem("small_split")
        x_hi, x_lo, x2_lo, w_hi, w_lo = sem("x_hi"), sem("x_lo"), sem("x2_lo"), sem("w_hi"), sem("w_lo")
        adj_hi, adj_lo, gnn_done, acc_done = sem("adj_hi"), sem("adj_lo"), sem("gnn_done"), sem("acc_done")
        h_hi, h_split, lay_done = sem("h_hi"), sem("h_split"), sem("lay_done")
        merge_psum, merge_sb, merge_rows = sem("merge_psum"), sem("merge_sb"), sem("merge_rows")
        xn_done, ln_step, sd_done = sem("xn_done"), sem("ln_step"), sem("sd_done")
        ln_rstd, ln_done = sem("ln_rstd"), sem("ln_done")
        lnT_psum, xT_hi, xT_lo = sem("lnT_psum"), sem("xT_hi"), sem("xT_lo")
        gates_psum, gates_sb, gates_rows = sem("gates_psum"), sem("gates_sb"), sem("gates_rows")
        top_step, diff_done, exp_done = sem("top_step"), sem("diff_done"), sem("exp_done")
        chosen_done, ranks, rank_step, slots_done = sem("chosen_done"), sem("ranks"), sem("rank_step"), sem("slots_done")
        scatters, scattered, table_step, tables = sem("scatters"), sem("scattered"), sem("table_step"), sem("tables")
        rows_in = [sem(f"rows_in{i}") for i in range(WR)]
        weights_in = [sem(f"weights_in{i}") for i in range(WR)]
        t_turned, t_xhi, t_xlo, t_up, t_relu = sem("t_turned"), sem("t_xhi"), sem("t_xlo"), sem("t_up"), sem("t_relu")
        t_hi, t_lo, t_down, t_y, t_rows = sem("t_hi"), sem("t_lo"), sem("t_down"), sem("t_y"), sem("t_rows")
        t_out = sem("t_out")
        t_stored = [sem(f"t_stored{i}") for i in range(2)]
        kept_in = [sem(f"kept_in{i}") for i in range(2)]
        gather_in = [sem(f"gather_in{i}") for i in range(2)]
        sum_step, summed = sem("sum_step"), sem("summed")
        locate_step, located = sem("locate_step"), sem("located")
        out_dma = [sem(f"out_dma{i}") for i in range(2)]

        LN_STEPS, TOP_STEPS, RANK_STEPS = 8, 5, 3

        def wait(eng, s, value):
            if not isinstance(value, int) or value > 0:
                eng.wait_ge(s, value)

        def at_block(t, j):
            return t[j] if isinstance(j, int) else t[bass.ds(j, 1)].rearrange("o p n -> (o p) n")

        def bodies(eng, body):
            body(0, 0, plan(0))
            body(1, 1, plan(1))
            with eng.Fori(1, GROUP_BLOCKS[0] // 2) as k:
                for par in range(2):
                    body(2 * k + par, par, plan(2))
            for b in range(GROUP_BLOCKS[0], BLOCKS + 1):
                body(b, b % 2, plan(b))

        def tile_turn(i, returned, turned, main, former):
            def has(k):
                return not isinstance(i, int) or 0 <= i + k < ALL_TILES

            if has(-2):
                returned(i - 2)
            if has(1):
                turned(i + 1)
            if has(0):
                main(i)
            if has(-1):
                former(i - 1)

        def group(i):
            return 0 if isinstance(i, int) and i < FIRST_TILE[1] else 1

        def last_tiles(eng, turn, end=None):
            lo, hi = FIRST_TILE[1], ALL_TILES
            for i in range(lo, lo + 2):
                turn(i, i % WR)
            with eng.Fori(0, (hi - lo) // WR - 1) as k:
                for u in range(WR):
                    turn(WR * k + (lo + 2 + u), (lo + 2 + u) % WR)
                    if end:
                        end(k, u)
            for i in range(hi - 2, hi + 2):
                turn(i, i % WR)

        block = ctx.enter_context(nc.Block())

        @block.sync
        def _(sp):
            def load_x(q):
                if q >= 2:
                    sp.wait_ge(x_lo, q - 1)
                    sp.wait_ge(x2_lo, q - 1)
                sp.dma_start(th[:, q % 2, :], x[q]).then_inc(x_in[q % 2], 16)
                sp.dma_start(rawx2[:, q % 2, :], x2[q]).then_inc(x2_in[q % 2], 16)

            def load_adj(b, c):
                wait(sp, adj_lo, KT * b + KC * (c - RAW) + KC)
                sp.dma_start(raw[:, c % RAW, :], adj[b, c] if isinstance(b, int) else
                             adj[bass.ds(b, 1), c].rearrange("o p n -> (o p) n")).then_inc(raw_in[c % RAW], 16)

            def fill_behind(g):
                sp.wait_ge(const_step, 3)
                sp.wait_ge(ends_known, g + 1)
                for e in range(E):
                    at = sp.value_load(ends_at[g][0:1, e:e + 1], min_val=0, max_val=E * STRIDE[g] - TS)
                    sp.dma_start(xs[g][bass.ds(at, TS), :].rearrange("(p a) d -> p a d", a=TA),
                                 zero[:, :].rearrange("p (o d) -> p o d", o=1).to_broadcast([P, TA, D]))\
                        .then_inc(zero_out, 16)

            def tile_rows(base):
                return base.rearrange("(p a) d -> p (a d)", a=TA)

            def load_rows(i, slot, g):
                at = sp.value_load(tab[g][0:1, 0, i_of(i, g)], min_val=0, max_val=E * STRIDE[g] - TS)
                wait(sp, t_turned, i - WR + 1)
                sp.dma_start(xr[:, slot, :], tile_rows(xs[g][bass.ds(at, TS), :])).then_inc(rows_in[slot], 16)

            def load_weights(i, slot, g):
                e = sp.value_load(tab[g][0:1, 1, i_of(i, g)], min_val=0, max_val=E - 1)
                wait(sp, t_y, i - WR + 1)
                sp.dma_start(f(wbuf[:, slot, :]), wset[bass.ds(e, 1)].rearrange("o p n -> (o p) n"))\
                    .then_inc(weights_in[slot], 16)
                sp.dma_start(bbuf[:, slot, :], bset[bass.ds(e, 1)].rearrange("o p n -> (o p) n"))\
                    .then_inc(weights_in[slot], 16)

            def i_of(i, g):
                return slice(i - FIRST_TILE[g], i - FIRST_TILE[g] + 1) if isinstance(i, int) \
                    else bass.ds(i - FIRST_TILE[g], 1)

            def store_rows(i, slot, g):
                sp.wait_ge(t_out, i + 1)
                k = i - FIRST_TILE[g]
                dst = ys[g][k * TS:k * TS + TS, :] if isinstance(i, int) else ys[g][bass.ds(k * TS, TS), :]
                sp.dma_start(tile_rows(dst), tyr[:, slot % 2, :]).then_inc(t_stored[slot % 2], 16)

            def group_ready(g):
                sp.wait_ge(tables, g + 1)
                sp.wait_ge(scattered, 16 * TOP * JT * (GROUP_BLOCKS[0] if g == 0 else BLOCKS))
                sp.wait_ge(zero_out, 16 * E * (g + 1))

            def tiles(i, slot):
                if not isinstance(i, int) or i + 2 < ALL_TILES:
                    if isinstance(i, int) and i + 2 == FIRST_TILE[1]:
                        group_ready(1)
                    load_rows(i + 2, (slot + 2) % WR, group(i + 2))
                    load_weights(i + 2, (slot + 2) % WR, group(i + 2))
                if not isinstance(i, int) or i >= 2:
                    store_rows(i - 2, (slot - 2) % WR, group(i - 2))

            load_x(0)
            for c in range(2):
                load_adj(0, c)
            sp.dma_start(smallS[:, :], small).then_inc(small_in, 16)
            sp.dma_start(wgS[:, :], wg).then_inc(small_in, 16)
            load_x(1)
            for c in range(2, NC):
                load_adj(0, c)
                if c % 2 == 0 and 2 + (c - 2) // 2 < BLOCKS:
                    load_x(2 + (c - 2) // 2)
            for c in range(RAW):
                load_adj(1, c)

            def body(b, par, turns):
                if isinstance(b, int) and b == 0:
                    return
                for t, (g, _, stages, tile) in enumerate(turns):
                    if g is not None and g % KC == 0 and g // KC + RAW < NC:
                        load_adj(b, g // KC + RAW)
                    elif g is not None and g % KC == 0 and (not isinstance(b, int) or b < BLOCKS - 1):
                        load_adj(b + 1, g // KC + RAW - NC)
                    if t == 2:
                        wait(sp, xn_done, b - 1)
                        sp.dma_start(xres[:, :], at_block(x, b - 1)).then_inc(xres_in, 16)
                    if tile == 0:
                        fill_behind(0)
                        group_ready(0)
                        sp.wait_ge(wset_out, 16 * E)
                        for i in range(2):
                            load_rows(i, i, 0)
                            load_weights(i, i, 0)
                    if tile is not None:
                        tiles(tile, tile % WR)
                    if g == 28 or (g is None and "close" in stages):
                        sp.wait_ge(slots_done, b)
                        sp.dma_start(at_block(keepd, b - 1), keep[:, :]).then_inc(keep_out, 16)
                    if g is None and "close" in stages:
                        fill_behind(1)

            bodies(sp, body)
            last_tiles(sp, tiles)
            for i in range(2):
                sp.wait_ge(out_dma[i], 16 * (BLOCKS // 2))

        @block.gpsimd
        def _(pool):
            def triangle(dst, compare, step):
                nc.gpsimd.affine_select(out=dst, in_=dst, compare_op=compare, fill=1.0, base=0, pattern=[[step, P]],
                                        channel_multiplier=-step).then_inc(consts, 1)

            nc.gpsimd.memset(ident[:, :], 0.0).then_inc(const_step, 1)
            nc.gpsimd.memset(earlier[:, :], 0.0).then_inc(const_step, 1)
            nc.gpsimd.memset(zero[:, :], 0.0).then_inc(const_step, 1)
            nc.gpsimd.memset(ones[:, :], 1.0).then_inc(const_step, 1)
            nc.gpsimd.memset(upto[:, :, :], 1.0).then_inc(const_step, 1)
            pool.wait_ge(const_step, 5)
            triangle(ident[:, :], ALU.not_equal, -1)
            nc.gpsimd.affine_select(out=earlier[:, :], in_=earlier[:, :], compare_op=ALU.is_ge, fill=1.0, base=0,
                                    pattern=[[-1, P]], channel_multiplier=1).then_inc(consts, 1)
            nc.gpsimd.affine_select(out=upto[:, :, :], in_=upto[:, :, :], compare_op=ALU.is_ge, fill=0.0, base=0,
                                    pattern=[[1, E], [-1, E]], channel_multiplier=0).then_inc(consts, 1)

            def counting(dst, pattern):
                nc.gpsimd.iota(dst, pattern=pattern, base=0, channel_multiplier=0,
                               allow_small_or_imprecise_dtypes=True).then_inc(consts, 1)

            counting(iota[:, :, :], [[0, JT], [1, E]])
            for g in range(2):
                counting(bases[g][:, :], [[STRIDE[g], E]])
            counting(nextslot[:, :], [[STRIDE[0], E]])
            counting(steps_of[:, :, :], [[0, E], [TS, MT]])
            counting(tilei[:, :], [[1, TILES[0]]])

            def x2_low(q):
                pool.wait_ge(x_hi, 2 * q + 2)
                nc.gpsimd.tensor_tensor(Xl[:, JT * q:JT * q + JT, D:2 * D], rows(rawx2[:, q % 2, :]),
                                        f(Xh[:, JT * q:JT * q + JT, D:2 * D]), ALU.subtract).then_inc(x2_lo, 1)

            def w_low(i):
                pool.wait_ge(w_hi, i + 1)
                if i == 0:
                    hi, lo = Wsh[:, :], Wsl[:, :]
                    nc.gpsimd.tensor_tensor(lo, stage_w[:, 0, :], f(hi), ALU.subtract).then_inc(w_lo, 1)
                    return
                w = wbuf[:, (i - 1) % WR, :].rearrange("p (m h n) -> p m h n", m=2, h=2)
                src = stage_w[:, i % 2, :].rearrange("p (m n) -> p m n", m=2)
                nc.gpsimd.tensor_tensor(w[:, :, 1, :], src, f(w[:, :, 0, :]), ALU.subtract).then_inc(w_lo, 1)

            def load_w(i):
                if i >= 2:
                    pool.wait_ge(w_lo, i - 1)
                pool.dma_start(stage_w[:, i % 2, :], wsm if i == 0 else wraw[i - 1]).then_inc(w_in[i % 2], 16)

            def store_w(e):
                pool.wait_ge(w_lo, e + 2)
                pool.dma_start(wset[e], f(wbuf[:, e % WR, :])).then_inc(wset_out, 16)

            def scatter(j, g):
                pool.wait_ge(slots_done, j + 1)
                pool.sem_inc(scatters, 1)
                for i in range(TOP):
                    for t in range(JT):
                        pool.indirect_dma_start(
                            out=xs[g][:, :], in_=lnr[:, t * D:t * D + D], in_offset=None,
                            out_offset=bass.IndirectOffsetOnAxis(ap=slots[:, i * JT + t:i * JT + t + 1], axis=0)
                        ).then_inc(scattered, 16)

            def load_kept(j, par):
                pool.wait_ge(keep_out, 16 * BLOCKS)
                pool.dma_start(keepS[:, par, :], keepd[j]).then_inc(kept_in[par], 16)

            def gather(j, par, g):
                for k in range(2):
                    pool.wait_ge(t_stored[k], 16 * (FIRST_TILE[g] + TILES[g]) // 2)
                pool.wait_ge(located, j + 1)
                wait(pool, summed, j - 1)
                for i in range(TOP * JT):
                    pool.indirect_dma_start(
                        out=gathered[:, par, i, :], out_offset=None, in_=ys[g][:, :],
                        in_offset=bass.IndirectOffsetOnAxis(ap=resrow[:, par, i:i + 1], axis=0)
                    ).then_inc(gather_in[par], 16)

            def store(j, par):
                pool.wait_ge(summed, j + 1)
                pool.dma_start(out[j], keepS[:, par, 0:NB]).then_inc(out_dma[par], 16)

            x2_low(0)
            for i in range(2):
                load_w(i)
            for b in range(2):
                for s in range(KT):
                    if b == 0 and s % 4 == 0 and s // 4 + 1 < BLOCKS:
                        x2_low(s // 4 + 1)
                    if s in SPLIT_W[b]:
                        i = SPLIT_W[b][s]
                        w_low(i)
                        if i > 0:
                            store_w(i - 1)
                        if i + 2 < E + 1:
                            load_w(i + 2)
            scatter(0, 0)
            with pool.Fori(1, GROUP_BLOCKS[0] - 1) as j:
                scatter(j, 0)
            scatter(GROUP_BLOCKS[0] - 1, 0)
            for j in range(GROUP_BLOCKS[0], BLOCKS):
                scatter(j, 1)
            for par in range(2):
                load_kept(par, par)
            for j in range(0, BLOCKS, 2):
                for par in range(2):
                    gather(j + par, par, 0 if j < GROUP_BLOCKS[0] else 1)
                for par in range(2):
                    store(j + par, par)
                    if j + par + 2 < BLOCKS:
                        pool.wait_ge(out_dma[par], 16 * (j // 2 + 1))
                        load_kept(j + par + 2, par)

        @block.tensor
        def _(pe):
            def three(ps, wh, wl, ih, il, start, stop):
                pe.matmul(ps, wh, ih, start=start, stop=False)
                pe.matmul(ps, wh, il, start=False, stop=False)
                return pe.matmul(ps, wl, ih, start=False, stop=stop)

            def gnn(b, par, s):
                if isinstance(b, int) and b == 0 and s % 4 == 0:
                    pe.wait_ge(x_lo, s // 4 + 1)
                    pe.wait_ge(x2_lo, s // 4 + 1)
                pe.wait_ge(adj_lo, KT * b + s + 1)
                for half in range(2):
                    if s == 0 and not (isinstance(b, int) and b < 2):
                        pe.wait_ge(h_split, 8 * (b - 2) + half + 1)
                    at = slice(half * D, half * D + D)
                    last = three(sums[par][half][:, :], Xh[:, s, at], Xl[:, s, at], Ah[:, s % RING, :],
                                 Al[:, s % RING, :], s == 0, s == KT - 1)
                    if s == KT - 1 and half == 0:
                        last.then_inc(acc_done, 1)
                last.then_inc(gnn_done, 1)

            def turn_rows(dst, src):
                for t in range(JT):
                    at = slice(t * P, t * P + P)
                    last = pe.transpose(dst[:, at], src[:, at], ident[:, :])
                return last

            def stage(name, j):
                if name.startswith("layer"):
                    l = int(name[5:])
                    for half in range(2):
                        pe.wait_ge(h_split, 8 * j + 2 * (l - 1) + half + 1)
                        at = slice((half * LAYERS + l - 1) * D, (half * LAYERS + l) * D)
                        three(lay[half][:, :], Wsh[:, at], Wsl[:, at], lh[:, half, :], ll[:, half, :], True, True)\
                            .then_inc(lay_done, 1)
                elif name == "merge":
                    for half in range(2):
                        pe.wait_ge(h_split, 8 * j + 6 + half + 1)
                        at = slice((2 * LAYERS + half) * D, (2 * LAYERS + half + 1) * D)
                        last = three(lay[0][:, :], Wsh[:, at], Wsl[:, at], lh[:, half, :], ll[:, half, :],
                                     half == 0, half == 1)
                    last.then_inc(merge_psum, 1)
                elif name == "rows":
                    pe.wait_ge(merge_sb, j + 1)
                    turn_rows(lay[1], hbuf[:, 0, :]).then_inc(merge_rows, 1)
                elif name == "normT":
                    pe.wait_ge(ln_done, BLOCKS + j + 1)
                    turn_rows(lay[0], lnr).then_inc(lnT_psum, 1)
                elif name == "gates":
                    pe.wait_ge(xT_lo, j + 1)
                    three(lay[1][0:E, :], wgh[:, :], wgl[:, :], xTh[:, :], xTl[:, :], True, True)\
                        .then_inc(gates_psum, 1)
                elif name == "top_a":
                    pe.wait_ge(gates_sb, j + 1)
                    for t in range(JT):
                        last = pe.matmul(lay[0][:, t * E:t * E + E], hbuf[0:E, 1, t * P:t * P + P],
                                         ident[0:E, 0:E], start=True, stop=True)
                    last.then_inc(gates_rows, 1)
                elif name == "rank":
                    pe.wait_ge(chosen_done, j + 1)
                    pe.matmul(lay[1][:, 0:(JT + 1) * E], earlier[:, :], chosen[:, :], start=True, stop=False)
                    for t in range(JT):
                        m = JT - t
                        src = chosen[:, t * E:t * E + E].rearrange("p (o e) -> p o e", o=1).to_broadcast([P, m, E])
                        last = pe.matmul(lay[1][:, (t + 1) * E:(JT + 1) * E].rearrange("p (o e) -> p o e", e=E),
                                         ones[:, :], src, start=False, stop=(t == JT - 1))
                    last.then_inc(ranks, 1)

            def turn_tile(i, slot):
                pe.wait_ge(rows_in[slot], 16 * of_ring(i, slot))
                wait(pe, t_xlo, i)
                for a in range(TA):
                    at = slice(a * P, a * P + P)
                    last = pe.transpose(tin[:, at], xr[:, slot, at], ident[:, :])
                last.then_inc(t_turned, 1)

            def of_ring(i, slot):
                return i // WR + 1 if isinstance(i, int) else (i - slot) // WR + 1

            def up_tile(i, slot):
                pe.wait_ge(weights_in[slot], 32 * of_ring(i, slot))
                pe.wait_ge(t_xlo, i + 1)
                for pair in range(2):
                    wait(pe, t_relu, 2 * i - 1 + pair)
                    for half in range(2):
                        c = 2 * pair + half
                        last = three(upP[pair][:, half * TS:half * TS + TS],
                                     wbuf[:, slot, c * P:c * P + P], wbuf[:, slot, HID + c * P:HID + c * P + P],
                                     tTh[:, slot % 2, :], tTl[:, slot % 2, :], True, True)
                    last.then_inc(t_up, 1)

            def down_tile(i, slot):
                pe.wait_ge(t_lo, 2 * i + 2)
                wait(pe, t_out, i)
                for c in range(HC):
                    hid = (slice(None), slot % 2, c // 2, slice((c % 2) * TS, (c % 2) * TS + TS))
                    last = three(ty[:, 0:TS], wbuf[:, slot, 2 * HID + c * P:2 * HID + c * P + P],
                                 wbuf[:, slot, 3 * HID + c * P:3 * HID + c * P + P], tHh[hid], tHl[hid],
                                 c == 0, c == HC - 1)
                last.then_inc(t_down, 1)

            def return_tile(i, slot):
                pe.wait_ge(t_y, i + 1)
                for a in range(TA):
                    last = pe.transpose(ty[:, TS + a * P:TS + a * P + P], tyT[:, slot % 2, a * P:a * P + P], ident[:, :])
                last.then_inc(t_rows, 1)

            def tiles(i, slot):
                tile_turn(i, lambda k: return_tile(k, (slot - 2) % WR), lambda k: turn_tile(k, (slot + 1) % WR),
                          lambda k: up_tile(k, slot), lambda k: down_tile(k, (slot - 1) % WR))

            def body(b, par, turns):
                if isinstance(b, int) and b == 1:
                    pe.wait_ge(w_lo, 1)
                    pe.wait_ge(small_split, 3)
                for g, _, stages, tile in turns:
                    for name in stages:
                        if name not in ("h0", "norm_a", "norm_b", "top_b", "close"):
                            stage(name, b - 1)
                    if tile == 0:
                        turn_tile(0, 0)
                    if g is not None:
                        gnn(b, par, g)
                    if tile is not None:
                        tiles(tile, tile % WR)

            pe.wait_ge(consts, 9)
            bodies(pe, body)
            last_tiles(pe, tiles)

        @block.scalar
        def _(act):
            def high(dst, src):
                return nc.scalar.activation(dst, src, ACT.Copy)

            def adj_high(b, k):
                c, slot = k // KC, (k // KC) % RAW
                act.wait_ge(raw_in[slot], 16 * (NC // RAW * b + c // RAW + 1))
                wait(act, gnn_done, KT * b + k - RING + 1)
                high(Ah[:, k % RING, :], raw[:, slot, (k % KC) * NB:(k % KC + 1) * NB]).then_inc(adj_hi, 1)

            def x_high(q):
                at = slice(JT * q, JT * q + JT)
                act.wait_ge(x2_in[q % 2], 16 * (q // 2 + 1))
                high(Xh[:, at, D:2 * D], rows(rawx2[:, q % 2, :])).then_inc(x_hi, 1)
                act.wait_ge(ln_step, LN_STEPS * q + 4)
                act.activation(nrm[:, 1, :], nrm[:, 0, :], ACT.Sqrt).then_inc(sd_done, 1)
                act.wait_ge(ln_done, q + 1)
                high(Xh[:, at, 0:D], rows(th[:, q % 2, :])).then_inc(x_hi, 1)

            def w_high(i):
                act.wait_ge(w_in[i % 2], 16 * (i // 2 + 1))
                if i == 0:
                    high(Wsh[:, :], stage_w[:, 0, :]).then_inc(w_hi, 1)
                    return
                if i > WR:
                    act.wait_ge(wset_out, 16 * (i - WR))
                w = wbuf[:, (i - 1) % WR, :].rearrange("p (m h n) -> p m h n", m=2, h=2)
                high(w[:, :, 0, :], stage_w[:, i % 2, :].rearrange("p (m n) -> p m n", m=2)).then_inc(w_hi, 1)

            def stage(name, j, par):
                if name == "h0":
                    wait(act, merge_psum, j)
                    for half in range(2):
                        if half == 0:
                            act.wait_ge(acc_done, j + 1)
                        else:
                            act.wait_ge(gnn_done, KT * j + KT)
                        nc.scalar.activation(lh[:, half, :], sums[par][half][:, :], ACT.Copy,
                                             scale=eps1p[:, half:half + 1]).then_inc(h_hi, 1)
                elif name.startswith("layer"):
                    l = int(name[5:])
                    for half in range(2):
                        act.wait_ge(lay_done, 6 * j + 2 * (l - 1) + half + 1)
                        bias = smallS[:, C_CONV_B + half * LAYERS + l - 1:C_CONV_B + half * LAYERS + l]
                        nc.scalar.activation(hbuf[:, half, :], lay[half][:, :], ACT.Relu, bias=bias)
                        nc.scalar.activation(lh[:, half, :], lay[half][:, :], ACT.Relu, bias=bias)\
                            .then_inc(h_hi, 1)
                elif name == "merge":
                    act.wait_ge(merge_psum, j + 1)
                    nc.scalar.activation(hbuf[:, 0, :], lay[0][:, :], ACT.Identity,
                                         bias=smallS[:, C_BM:C_BM + 1]).then_inc(merge_sb, 1)
                elif name == "norm_b":
                    act.wait_ge(ln_step, LN_STEPS * (BLOCKS + j) + 4)
                    act.activation(nrm[:, 1, :], nrm[:, 0, :], ACT.Sqrt).then_inc(sd_done, 1)
                elif name == "normT":
                    act.wait_ge(lnT_psum, j + 1)
                    wait(act, gates_psum, j)
                    high(xTh[:, :], lay[0][:, :]).then_inc(xT_hi, 1)
                elif name == "gates":
                    act.wait_ge(gates_psum, j + 1)
                    nc.scalar.activation(hbuf[0:E, 1, :], lay[1][0:E, :], ACT.Identity,
                                         bias=smallS[0:E, C_BG:C_BG + 1]).then_inc(gates_sb, 1)
                elif name == "top_b":
                    act.wait_ge(diff_done, j + 1)
                    nc.scalar.activation(prob[:, 1, :], prob[:, 0, :], ACT.Exp).then_inc(exp_done, 1)

            def turned_tile(i, slot):
                act.wait_ge(t_turned, i + 1)
                wait(act, t_up, 2 * (i - 1))
                high(tTh[:, slot % 2, :], tin[:, 0:TS]).then_inc(t_xhi, 1)

            def relu_tile(i, slot):
                for pair in range(2):
                    wait(act, t_lo, 2 * (i - 1) + pair + 1)
                    act.wait_ge(t_up, 2 * i + pair + 1)
                    for half in range(2):
                        c, at = 2 * pair + half, slice(half * TS, half * TS + TS)
                        last = nc.scalar.activation(th[:, pair, at], upP[pair][:, at], ACT.Relu,
                                                    bias=bbuf[:, slot, c:c + 1])
                    last.then_inc(t_relu, 1)

            def sum_tile(i, slot):
                wait(act, t_rows, i - 1)
                act.wait_ge(t_down, i + 1)
                nc.scalar.activation(tyT[:, slot % 2, :], ty[:, 0:TS], ACT.Identity,
                                     bias=bbuf[:, slot, HC:HC + 1]).then_inc(t_y, 1)

            def tiles(i, slot):
                tile_turn(i, lambda k: None, lambda k: turned_tile(k, (slot + 1) % WR),
                          lambda k: relu_tile(k, slot), lambda k: sum_tile(k, (slot - 1) % WR))

            def body(b, par, turns):
                first = isinstance(b, int) and b == 0
                for g, split, stages, tile in turns:
                    for name in stages:
                        stage(name, b - 1, 1 - par)
                    if tile == 0:
                        turned_tile(0, 0)
                    for k in split:
                        adj_high(b, k)
                    if first:
                        if g % 4 == 0 and g // 4 + 1 < BLOCKS:
                            x_high(g // 4 + 1)
                    if isinstance(b, int) and g in SPLIT_W.get(b, {}):
                        w_high(SPLIT_W[b][g])
                    if tile is not None:
                        tiles(tile, tile % WR)

            for k in range(AHEAD - 1):
                adj_high(0, k)
            x_high(0)
            adj_high(0, AHEAD - 1)
            act.wait_ge(small_in, 32)
            high(wgh[:, :], wgS[:, :]).then_inc(small_split, 1)
            bodies(act, body)
            last_tiles(act, tiles)

        @block.vector
        def _(dve):
            def low(dst, src, hi):
                return nc.vector.tensor_tensor(dst, src, f(hi), ALU.subtract)

            def adj_low(b, k):
                dve.wait_ge(adj_hi, KT * b + k + 1)
                low(Al[:, k % RING, :], raw[:, (k // KC) % RAW, (k % KC) * NB:(k % KC + 1) * NB],
                    Ah[:, k % RING, :]).then_inc(adj_lo, 1)

            def variance(use, src):
                base = LN_STEPS * use
                for t in range(JT):
                    last = nc.vector.bn_stats(stats[:, t, :], src[:, t * D:t * D + D])
                last.then_inc(ln_step, 1)
                dve.wait_ge(ln_step, base + 1)
                nc.vector.tensor_tensor(mom[:, 0, :], stats[:, :, 1], stats[:, :, 4], ALU.add)
                nc.vector.tensor_tensor(mom[:, 1, :], stats[:, :, 1], stats[:, :, 4], ALU.subtract)
                nc.vector.tensor_tensor(mom[:, 2, :], stats[:, :, 2], stats[:, :, 5], ALU.add).then_inc(ln_step, 1)
                dve.wait_ge(ln_step, base + 2)
                nc.vector.tensor_scalar(mean[:, :], mom[:, 0, :], 0.5, None, ALU.mult)
                nc.vector.tensor_tensor(mom[:, 3, :], mom[:, 1, :], mom[:, 1, :], ALU.mult)
                nc.vector.tensor_scalar(mom[:, 4, :], mom[:, 2, :], 1.0 / D, EPS, ALU.mult, ALU.add)\
                    .then_inc(ln_step, 1)
                dve.wait_ge(ln_step, base + 3)
                nc.vector.scalar_tensor_tensor(out=nrm[:, 0, :], in0=mom[:, 3, :], scalar=0.25, in1=mom[:, 4, :],
                                               op0=ALU.mult, op1=ALU.add).then_inc(ln_step, 1)

            def normalise(use, dst, src):
                base = LN_STEPS * use
                dve.wait_ge(sd_done, use + 1)
                nc.vector.reciprocal(nrm[:, 2, :], nrm[:, 1, :]).then_inc(ln_step, 1)
                dve.wait_ge(ln_step, base + 5)
                nc.vector.tensor_tensor(nrm[:, 3, :], nrm[:, 2, :], nrm[:, 2, :], ALU.mult).then_inc(ln_step, 1)
                dve.wait_ge(ln_step, base + 6)
                nc.vector.tensor_tensor(nrm[:, 4, :], nrm[:, 3, :], nrm[:, 0, :], ALU.mult).then_inc(ln_step, 1)
                dve.wait_ge(ln_step, base + 7)
                nc.vector.tensor_scalar(nrm[:, 3, :], nrm[:, 4, :], -0.5, 1.5, ALU.mult, ALU.add).then_inc(ln_step, 1)
                dve.wait_ge(ln_step, base + 8)
                nc.vector.tensor_tensor(nrm[:, 5, :], nrm[:, 3, :], nrm[:, 2, :], ALU.mult).then_inc(ln_rstd, 1)
                dve.wait_ge(ln_rstd, use + 1)
                for t in range(JT):
                    at = slice(t * D, t * D + D)
                    last = nc.vector.tensor_scalar(dst[:, at], src[:, at], mean[:, t:t + 1], nrm[:, 5, t:t + 1],
                                                   ALU.subtract, ALU.mult)
                last.then_inc(ln_done, 1)

            def x_prepare(q):
                at = slice(JT * q, JT * q + JT)
                dve.wait_ge(x_in[q % 2], 16 * (q // 2 + 1))
                variance(q, th[:, q % 2, :])
                normalise(q, th[:, q % 2, :], th[:, q % 2, :])
                dve.wait_ge(x_hi, 2 * q + 2)
                low(Xl[:, at, 0:D], rows(th[:, q % 2, :]), Xh[:, at, 0:D]).then_inc(x_lo, 1)

            def stage(name, j, par):
                if name == "h0":
                    for half in range(2):
                        dve.wait_ge(h_hi, 8 * j + half + 1)
                        nc.vector.scalar_tensor_tensor(out=ll[:, half, :], in0=sums[par][half][:, :],
                                                       scalar=eps1p[:, half:half + 1], in1=f(lh[:, half, :]),
                                                       op0=ALU.mult, op1=ALU.subtract).then_inc(h_split, 1)
                elif name.startswith("layer"):
                    l = int(name[5:])
                    for half in range(2):
                        dve.wait_ge(h_hi, 8 * j + 2 * l + half + 1)
                        low(ll[:, half, :], hbuf[:, half, :], lh[:, half, :]).then_inc(h_split, 1)
                elif name == "rows":
                    dve.wait_ge(merge_rows, j + 1)
                    dve.wait_ge(xres_in, 16 * j + 16)
                    wait(dve, keep_out, 16 * j)
                    nc.vector.tensor_tensor(keep[:, 0:NB], lay[1][:, :], xres[:, :], ALU.add).then_inc(xn_done, 1)
                elif name == "norm_a":
                    dve.wait_ge(xn_done, j + 1)
                    variance(BLOCKS + j, keep)
                elif name == "norm_b":
                    wait(dve, scattered, 16 * TOP * JT * j)
                    normalise(BLOCKS + j, lnr, keep)
                elif name == "normT":
                    dve.wait_ge(xT_hi, j + 1)
                    low(xTl[:, :], lay[0][:, :], xTh[:, :]).then_inc(xT_lo, 1)
                elif name == "top_a":
                    base = TOP_STEPS * j
                    dve.wait_ge(gates_rows, j + 1)
                    scores = lay[0][:, 0:JT * E].rearrange("p (j e) -> p j e", j=JT)
                    nc.vector.tensor_copy(gS[:, :, :], scores)
                    for t in range(JT):
                        last = nc.vector.max(top[:, t, :], scores[:, t, :])
                    last.then_inc(top_step, 1)
                    dve.wait_ge(top_step, base + 1)
                    nc.vector.tensor_tensor(prob[:, 0, :], top[:, :, 1], top[:, :, 0], ALU.subtract)\
                        .then_inc(diff_done, 1)
                    for t in range(JT):
                        last = nc.vector.max_index(topi[:, t, :], top[:, t, :], gS[:, t, :])
                    last.then_inc(top_step, 1)
                    dve.wait_ge(top_step, base + 2)
                    nc.vector.tensor_copy(topf[:, :, :], topi[:, :, 0:2]).then_inc(top_step, 1)
                elif name == "top_b":
                    base = TOP_STEPS * j
                    dve.wait_ge(exp_done, j + 1)
                    nc.vector.tensor_scalar(prob[:, 2, :], prob[:, 1, :], 1.0, None, ALU.add).then_inc(top_step, 1)
                    dve.wait_ge(top_step, base + 4)
                    nc.vector.reciprocal(keep_p[:, 0, :], prob[:, 2, :])
                    for i in range(TOP):
                        last = nc.vector.tensor_tensor(by_expert(chose[:, i, :]), iota[:, :, :],
                                                       topf[:, :, i:i + 1].to_broadcast([P, JT, E]), ALU.is_equal)
                    last.then_inc(top_step, 1)
                    dve.wait_ge(top_step, base + 5)
                    nc.vector.tensor_tensor(keep_p[:, 1, :], prob[:, 1, :], keep_p[:, 0, :], ALU.mult)
                    nc.vector.tensor_tensor(chosen[:, 0:JT * E], chose[:, 0, :], chose[:, 1, :], ALU.add)\
                        .then_inc(chosen_done, 1)
                elif name == "rank":
                    base = RANK_STEPS * j
                    dve.wait_ge(ranks, j + 1)
                    nc.vector.tensor_tensor(place[:, :, :], by_expert(lay[1][:, 0:JT * E]),
                                            nextslot[:, :].rearrange("p (o e) -> p o e", o=1)
                                            .to_broadcast([P, JT, E]), ALU.add).then_inc(rank_step, 1)
                    dve.wait_ge(rank_step, base + 1)
                    nc.vector.tensor_tensor(nextslot[:, :], lay[1][:, JT * E:(JT + 1) * E], nextslot[:, :], ALU.add)
                    for i in range(TOP):
                        last = nc.vector.tensor_tensor(by_expert(picked[:, i, :]), place[:, :, :],
                                                       by_expert(chose[:, i, :]), ALU.mult)
                    last.then_inc(rank_step, 1)
                    dve.wait_ge(rank_step, base + 2)
                    nc.vector.tensor_reduce(keep_slot, picked[:, :, :].rearrange("p i (j e) -> p (i j) e", e=E),
                                            AX.X, ALU.add).then_inc(rank_step, 1)
                    dve.wait_ge(rank_step, base + 3)
                    nc.vector.tensor_copy(slots[:, :], keep_slot).then_inc(slots_done, 1)
                elif name == "close":
                    close(0 if j < GROUP_BLOCKS[0] else 1)

            table_steps = [0]

            def close(g):
                n = TILES[g]

                def then(last):
                    table_steps[0] += 1
                    last.then_inc(table_step, 1)
                    dve.wait_ge(table_step, table_steps[0])

                def each(i):
                    return tt[:, i, 0:n]

                def wide(ap, shape):
                    return ap.rearrange("p (o e) -> p o e", o=1).to_broadcast(shape)

                tokens, tiles_of, ends, shifts = (count[:, i, :] for i in range(4))
                ge, ge_tiles = (by_expert(passed[:, i, 0:n * E]) for i in range(2))
                nc.vector.tensor_copy(ends_at[g][:, :], nextslot[0:1, :]).then_inc(ends_known, 1)
                then(nc.vector.tensor_tensor(tokens, nextslot[:, :], bases[g][:, :], ALU.subtract))
                if g == 0:
                    nc.vector.tensor_copy(nextslot[:, :], bases[1][:, :])
                then(nc.vector.tensor_tensor(wideM[:, :, :], tokens.rearrange("p (e o) -> p e o", o=1)
                                             .to_broadcast([P, E, MT]), steps_of[:, :, :], ALU.is_gt))
                then(nc.vector.tensor_reduce(tiles_of, wideM[:, :, :], AX.X, ALU.add))
                then(nc.vector.tensor_tensor(wide8[:, :, :], upto[:, :, :], wide(tiles_of, [P, E, E]), ALU.mult))
                then(nc.vector.tensor_reduce(ends, wide8[:, :, :], AX.X, ALU.add))
                nc.vector.tensor_tensor(tokens, ends, tiles_of, ALU.subtract)
                then(nc.vector.tensor_tensor(ge, tilei[:, 0:n].rearrange("p (i o) -> p i o", o=1)
                                             .to_broadcast([1, n, E]), wide(ends[0:1], [1, n, E]), ALU.is_ge))
                nc.vector.scalar_tensor_tensor(out=shifts, in0=tokens, scalar=float(TS), in1=bases[g][:, :],
                                               op0=ALU.mult, op1=ALU.subtract)
                then(nc.vector.tensor_tensor(ge_tiles, ge, wide(tiles_of[0:1], [1, n, E]), ALU.mult))
                nc.vector.tensor_copy(moved[g][:, 0:1], shifts[:, 0:1])
                nc.vector.tensor_tensor(moved[g][:, 1:E], shifts[:, 1:E], shifts[:, 0:E - 1], ALU.subtract)
                nc.vector.tensor_reduce(each(0), ge, AX.X, ALU.add)
                then(nc.vector.tensor_reduce(each(1), ge_tiles, AX.X, ALU.add))
                nc.vector.tensor_scalar(each(2), each(0), float(E), None, ALU.is_lt)
                nc.vector.tensor_scalar(each(4), each(0), float(STRIDE[g]), None, ALU.mult)
                then(nc.vector.tensor_tensor(each(3), tilei[:, 0:n], each(1), ALU.subtract))
                then(nc.vector.tensor_scalar(each(5), each(3), float(TS), None, ALU.mult))
                then(nc.vector.tensor_tensor(each(6), each(4), each(5), ALU.add))
                nc.vector.tensor_tensor(tab[g][:, 0, :], each(6), each(2), ALU.mult)
                nc.vector.tensor_tensor(tab[g][:, 1, :], each(0), each(2), ALU.mult).then_inc(tables, 1)

            def turned_tile(i, slot):
                dve.wait_ge(t_xhi, i + 1)
                low(tTl[:, slot % 2, :], tin[:, 0:TS], tTh[:, slot % 2, :]).then_inc(t_xlo, 1)

            def split_tile(i, slot):
                for pair in range(2):
                    wait(dve, t_down, i - 1)
                    dve.wait_ge(t_relu, 2 * i + pair + 1)
                    nc.vector.tensor_copy(tHh[:, slot % 2, pair, :], th[:, pair, :]).then_inc(t_hi, 1)
                    dve.wait_ge(t_hi, 2 * i + pair + 1)
                    low(tHl[:, slot % 2, pair, :], th[:, pair, :], tHh[:, slot % 2, pair, :]).then_inc(t_lo, 1)

            def return_tile(i, slot):
                par = slot % 2
                wait(dve, t_stored[par], 8 * (i - par))
                dve.wait_ge(t_rows, i + 1)
                nc.vector.tensor_copy(tyr[:, par, :], ty[:, TS:2 * TS]).then_inc(t_out, 1)

            def tiles(i, slot):
                tile_turn(i, lambda k: return_tile(k, (slot - 2) % WR), lambda k: turned_tile(k, (slot + 1) % WR),
                          lambda k: split_tile(k, slot), lambda k: None)

            def locate(j, par, g):
                dve.wait_ge(kept_in[par], 8 * (j - par) + 16)
                slot = keepS[:, par, NB + TOP * JT:KEEP]
                ge, move = (by_expert(beyond[:, i, :]) for i in range(2))
                nc.vector.tensor_tensor(ge, slot.rearrange("p (i o) -> p i o", o=1).to_broadcast([P, TOP * JT, E]),
                                        bases[g][:, :].rearrange("p (o e) -> p o e", o=1)
                                        .to_broadcast([P, TOP * JT, E]), ALU.is_ge).then_inc(locate_step, 1)
                dve.wait_ge(locate_step, 3 * j + 1)
                nc.vector.tensor_tensor(move, ge, moved[g][:, :].rearrange("p (o e) -> p o e", o=1)
                                        .to_broadcast([P, TOP * JT, E]), ALU.mult).then_inc(locate_step, 1)
                dve.wait_ge(locate_step, 3 * j + 2)
                nc.vector.tensor_reduce(rowf[:, :], move, AX.X, ALU.add).then_inc(locate_step, 1)
                dve.wait_ge(locate_step, 3 * j + 3)
                nc.vector.tensor_tensor(resrow[:, par, :], rowf[:, :], slot, ALU.add).then_inc(located, 1)

            def sum_up(j, par):
                dve.wait_ge(gather_in[par], 8 * TOP * JT * (j - par) + 16 * TOP * JT)
                for i in range(TOP):
                    for t in range(JT):
                        at = slice(t * D, t * D + D)
                        last = nc.vector.scalar_tensor_tensor(
                            out=keepS[:, par, at], in0=gathered[:, par, i * JT + t, :],
                            scalar=keepS[:, par, NB + i * JT + t:NB + i * JT + t + 1], in1=keepS[:, par, at],
                            op0=ALU.mult, op1=ALU.add)
                    if i == 0:
                        last.then_inc(sum_step, 1)
                        dve.wait_ge(sum_step, j + 1)
                last.then_inc(summed, 1)

            def body(b, par, turns):
                for g, split, stages, tile in turns:
                    for name in stages:
                        stage(name, b - 1, 1 - par)
                    if tile == 0:
                        turned_tile(0, 0)
                    for k in split:
                        adj_low(b, k)
                    if isinstance(b, int) and b == 0 and g % 4 == 0 and g // 4 + 1 < BLOCKS:
                        x_prepare(g // 4 + 1)
                    if tile is not None:
                        tiles(tile, tile % WR)

            for k in range(AHEAD - 1):
                adj_low(0, k)
            x_prepare(0)
            adj_low(0, AHEAD - 1)
            dve.wait_ge(small_in, 32)
            dve.wait_ge(small_split, 1)
            low(wgl[:, :], wgS[:, :], wgh[:, :]).then_inc(small_split, 1)
            nc.vector.tensor_scalar(eps1p[:, :], smallS[:, C_EPS:C_EPS + 2], 1.0, 1.0, ALU.add, ALU.add)\
                .then_inc(small_split, 1)
            nc.vector.memset(chosen[:, :], 0.0)
            dve.wait_ge(consts, 9)
            bodies(dve, body)
            last_tiles(dve, tiles,
                       lambda k, u: locate(2 * k + u, u, 0) if u < 2 else sum_up(2 * k + (u - 2), u - 2))
            for j in range(GROUP_BLOCKS[0], BLOCKS):
                locate(j, j % 2, 1)
            for j in range(GROUP_BLOCKS[0], BLOCKS):
                sum_up(j, j % 2)


def kernel(x, adj, L0_gnn_x2, L0_gnn_eps1, L0_gnn_eps2, L0_gnn_W1, L0_gnn_b1, L0_gnn_W2, L0_gnn_b2, L0_gnn_Wm,
           L0_gnn_bm, L0_ffn_Wg, L0_ffn_bg, L0_ffn_W1, L0_ffn_b1, L0_ffn_W2, L0_ffn_b2):
    import numpy as np
    import concourse.bacc as bacc
    from concourse.bass_utils import run_bass_kernel_spmd

    def row_blocks(a):
        return np.ascontiguousarray(np.asarray(a).reshape(BLOCKS, JT, P, D).transpose(0, 2, 1, 3)).reshape(BLOCKS, P, NB)

    adj_l = np.asarray(adj).reshape(BLOCKS, NB, NC, KC, P).transpose(0, 2, 4, 3, 1)
    adj_l = np.ascontiguousarray(adj_l).reshape(BLOCKS, NC, P, KC * NB)
    wm = np.asarray(L0_gnn_Wm)
    wsm = np.concatenate([np.asarray(w)[i].T for w in (L0_gnn_W1, L0_gnn_W2) for i in range(LAYERS)]
                         + [wm[:, 0:D].T, wm[:, D:2 * D].T], axis=1)
    w1 = np.asarray(L0_ffn_W1).transpose(0, 2, 1)
    w2 = np.asarray(L0_ffn_W2).reshape(E, D, HC, P).transpose(0, 3, 2, 1).reshape(E, P, HC * D)
    bset = np.zeros((E, P, 8), np.float32)
    bset[:, :, 0:HC] = np.asarray(L0_ffn_b1).reshape(E, HC, P).transpose(0, 2, 1)
    bset[:, :, HC] = np.asarray(L0_ffn_b2)

    small = np.zeros((P, C_ALL), np.float32)
    small[:, C_EPS] = np.asarray(L0_gnn_eps1)[0]
    small[:, C_EPS + 1] = np.asarray(L0_gnn_eps2)[0]
    small[:, C_CONV_B:C_CONV_B + LAYERS] = np.asarray(L0_gnn_b1).T
    small[:, C_CONV_B + LAYERS:C_CONV_B + 2 * LAYERS] = np.asarray(L0_gnn_b2).T
    small[:, C_BM] = np.asarray(L0_gnn_bm)
    small[0:E, C_BG] = np.asarray(L0_ffn_bg)
    arrays = {
        "adj_l": adj_l, "x_rows": row_blocks(x), "x2_rows": row_blocks(L0_gnn_x2),
        "wsm": np.ascontiguousarray(wsm), "wraw": np.ascontiguousarray(np.concatenate([w1, w2], axis=2)),
        "wg": np.ascontiguousarray(np.asarray(L0_ffn_Wg).T), "small": small, "bset": bset,
    }
    nc = bacc.Bacc("TRN2", target_bir_lowering=False, num_devices=1, dynamic_dma_scratch_size=4096)
    args = [nc.dram_tensor(n, a.shape, F32, kind="ExternalInput").ap() for n, a in arrays.items()]
    out = nc.dram_tensor("out_rows", (BLOCKS, P, NB), F32, kind="ExternalOutput").ap()
    wset = nc.dram_tensor("wset", (E, P, WS), F32, kind="Internal").ap()
    keepd = nc.dram_tensor("keepd", (BLOCKS, P, NB + 2 * TOP * JT), F32, kind="Internal").ap()
    xs = [nc.dram_tensor(f"slots{g}", (E * STRIDE[g], D), F32, kind="Internal").ap() for g in range(2)]
    ys = [nc.dram_tensor(f"results{g}", (TS * TILES[g], D), F32, kind="Internal").ap() for g in range(2)]
    gnn_mixture(nc, *args, out, wset, keepd, xs, ys)
    r = run_bass_kernel_spmd(nc, [arrays], core_ids=[0])
    got = np.asarray(r.results[0]["out_rows"])
    return got.reshape(BLOCKS, P, JT, D).transpose(0, 2, 1, 3).reshape(N, D)
```

```python
from contextlib import ExitStack

import concourse.bass as bass
from concourse import mybir

P = 128
N = 4096
D = 128
NB = 512
BLOCKS = N // NB
KT = N // P
JT = NB // P
E = 8
TOP = 2
HID = 512
HC = HID // P
LAYERS = 3
EPS = 1e-5

KC = 2
NC = KT // KC
RAW = 4
RING = 4
AHEAD = 3

TS = 256
TA = TS // P
GROUP_BLOCKS = (6, 2)
CAP = tuple(n * NB for n in GROUP_BLOCKS)
STRIDE = tuple(c + TS for c in CAP)
TILES = tuple((TOP * c // TS + E - 1 + 1) // 2 * 2 for c in CAP)
FIRST_TILE = (0, TILES[0])
ALL_TILES = sum(TILES)
WR = 4
WS = 2 * HID
BS = 8

F32 = mybir.dt.float32
F32R = mybir.dt.float32r
U32 = mybir.dt.uint32
I32 = mybir.dt.int32
ALU = mybir.AluOpType
ACT = mybir.ActivationFunctionType
AX = mybir.AxisListType

C_EPS, C_CONV_B, C_BM, C_BG = 0, 2, 8, 9
C_ALL = 10

CHAIN = {0: ["h0"], 2: ["layer1"], 5: ["layer2"], 8: ["layer3"], 11: ["merge"], 13: ["rows"], 14: ["norm_a"],
         15: ["norm_b"], 17: ["normT"], 19: ["gates"], 21: ["top_a"], 22: ["top_b"], 24: ["rank"], 26: ["close"]}
LAST_CHAIN = {0: ["h0"], 1: ["layer1"], 2: ["layer2"], 3: ["layer3"], 4: ["merge"], 5: ["rows"], 6: ["norm_a"],
              7: ["norm_b"], 8: ["normT"], 9: ["gates"], 10: ["top_a"], 11: ["top_b"], 12: ["rank"], 13: ["close"]}
IN_BODY_7 = 12
FIRST_STEP = 7
SPLIT_W = 26
X_AHEAD = 6
POOL_TILES = IN_BODY_7 + 12


def plan(b):
    if b == BLOCKS:
        return [(None, [], LAST_CHAIN.get(t, []), IN_BODY_7 + t) for t in range(TILES[0] - IN_BODY_7)]
    turns = []
    for t in range(KT):
        split = [t + AHEAD] if t + AHEAD < KT or b < BLOCKS - 1 else []
        stages = [x for x in CHAIN.get(t, []) if b > 0 and (x != "close" or b == GROUP_BLOCKS[0])]
        before, after = ((t + u - FIRST_STEP) * IN_BODY_7 // (KT - FIRST_STEP) for u in range(2))
        turns.append((t, split, stages, before if b == BLOCKS - 1 and before >= 0 and after > before else None))
    return turns


def x_parts(g):
    first = {q: max(0, JT * q - X_AHEAD) for q in range(1, BLOCKS)}
    return [(q, g - first[q]) for q in range(1, BLOCKS) if 0 <= g - first[q] < 3]


def gnn_mixture(nc, adj, x, x2, wsm, wraw, wg, small, out, keepd, xs, ys):
    with ExitStack() as ctx:
        def sb(name, shape, dt=F32):
            return ctx.enter_context(nc.sbuf_tensor(name, shape, dt))

        def sem(name):
            return ctx.enter_context(nc.semaphore(name))

        Wsh = sb("Wsh", [P, 2 * HID], F32R)
        Wsl = sb("Wsl", [P, 2 * HID], F32R)
        raw = sb("raw", [P, RAW, KC * NB])
        Ah = sb("Ah", [P, RING, NB], F32R)
        Al = sb("Al", [P, RING, NB], F32R)
        hbuf = sb("hbuf", [P, 2, NB])
        lh = sb("lh", [P, 2, NB], F32R)
        ll = sb("ll", [P, 2, NB], F32R)
        lnr = sb("lnr", [P, NB])
        KEEP = NB + 2 * TOP * JT
        keep = sb("keep", [P, KEEP])
        xres = sb("xres", [P, NB])
        xTh = sb("xTh", [P, NB], F32R)
        xTl = sb("xTl", [P, NB], F32R)
        wbuf = sb("wbuf", [P, WR, WS + BS])
        wsplit = [sb(f"wsplit{m}", [P, 2, 2, HID], F32R) for m in range(2)]
        xr = sb("xr", [P, WR, TS])
        tTh = sb("tTh", [P, 2, TS], F32R)
        tTl = sb("tTl", [P, 2, TS], F32R)
        th = sb("th", [P, 2, NB])
        tHh = sb("tHh", [P, 2, 2, NB], F32R)
        tHl = sb("tHl", [P, 2, 2, NB], F32R)
        tyT = sb("tyT", [P, 2, TS])
        tyr = sb("tyr", [P, 2, TS])
        rawx2 = sb("rawx2", [P, 2, NB])
        stage_w = sb("stage_w", [P, 2 * HID])
        smallS = sb("smallS", [P, C_ALL])
        eps1p = sb("eps1p", [P, 2])
        wgS = sb("wgS", [P, E])
        wgh = sb("wgh", [P, E], F32R)
        wgl = sb("wgl", [P, E], F32R)
        zero = sb("zero", [P, P])
        ident = sb("ident", [P, P])
        ones = sb("ones", [P, P])
        earlier = sb("earlier", [P, P])
        iota = sb("iota", [P, JT, E])
        stats = sb("stats", [P, JT, 6])
        mom = sb("mom", [P, 5, JT])
        mean = sb("mean", [P, JT])
        nrm = sb("nrm", [P, 6, JT])
        gS = sb("gS", [P, JT, E])
        top = sb("top", [P, JT, 8])
        topi = sb("topi", [P, JT, 8], U32)
        topf = sb("topf", [P, JT, TOP])
        prob = sb("prob", [P, 3, JT])
        chose = sb("chose", [P, TOP, JT * E])
        chosen = sb("chosen", [P, (JT + 1) * E])
        bases = [sb(f"base{g}", [P, E]) for g in range(2)]
        nextslot = sb("nextslot", [P, E])
        place = sb("place", [P, JT, E])
        picked = sb("picked", [P, TOP, JT * E])
        slots = sb("slots", [P, TOP * JT], U32)
        MT = CAP[0] // TS
        steps_of = sb("steps_of", [P, E, MT])
        upto = sb("upto", [P, E, E])
        count = sb("count", [P, 4, E])
        wide8 = sb("wide8", [P, E, E])
        wideM = sb("wideM", [P, E, MT])
        tilei = sb("tilei", [1, TILES[0]])
        passed = sb("passed", [1, 2, TILES[0] * E])
        tt = sb("tt", [1, 7, TILES[0]])
        tab = [sb(f"tab{g}", [1, 2, TILES[g]], I32) for g in range(2)]
        ends_at = [sb(f"ends_at{g}", [1, E], I32) for g in range(2)]
        moved = [sb(f"moved{g}", [P, E]) for g in range(2)]
        beyond = sb("beyond", [P, 2, GROUP_BLOCKS[0] * TOP * JT * E])
        rowf = sb("rowf", [P, GROUP_BLOCKS[0], TOP * JT])
        resrow = sb("resrow", [P, BLOCKS, TOP * JT], U32)

        with nc.sbuf_tensor("Xh", [P, KT, 2 * D], F32R) as Xh, nc.sbuf_tensor("Xl", [P, KT, 2 * D], F32R) as Xl:
            pass
        gathered = sb("gathered", [P, BLOCKS, TOP * JT, D])
        kept = sb("kept", [P, BLOCKS, KEEP])

        acc = [ctx.enter_context(nc.psum_tensor(f"acc{i}", [P, NB], F32)) for i in range(2)]
        lay = [ctx.enter_context(nc.psum_tensor(f"lay{i}", [P, NB], F32)) for i in range(2)]
        upP = [ctx.enter_context(nc.psum_tensor(f"up{i}", [P, NB], F32)) for i in range(2)]
        tin = ctx.enter_context(nc.psum_tensor("tin", [P, NB], F32))
        ty = ctx.enter_context(nc.psum_tensor("ty", [P, NB], F32))

        def f(ap):
            return ap.bitcast(F32)

        def rows(ap):
            return ap.rearrange("p (j d) -> p j d", j=JT)

        def by_expert(ap):
            return ap.rearrange("p (j e) -> p j e", e=E)

        keep_p = keep[:, NB:NB + TOP * JT].rearrange("p (i j) -> p i j", i=TOP)
        keep_slot = keep[:, NB + TOP * JT:KEEP]

        sums = [upP, acc]

        small_in = sem("small_in")
        x_in = [sem(f"x_in{i}") for i in range(2)]
        x2_in = [sem(f"x2_in{i}") for i in range(2)]
        raw_in = [sem(f"raw_in{i}") for i in range(RAW)]
        xres_in, w_in, zero_out, keep_out = sem("xres_in"), sem("w_in"), sem("zero_out"), sem("keep_out")
        ends_known = sem("ends_known")
        const_step, consts, small_split = sem("const_step"), sem("consts"), sem("small_split")
        x_hi, x_lo, x2_lo, w_hi, w_lo = sem("x_hi"), sem("x_lo"), sem("x2_lo"), sem("w_hi"), sem("w_lo")
        adj_hi, adj_lo, gnn_done, acc_done = sem("adj_hi"), sem("adj_lo"), sem("gnn_done"), sem("acc_done")
        h_hi, h_split, lay_done = sem("h_hi"), sem("h_split"), sem("lay_done")
        merge_psum, merge_sb, merge_rows = sem("merge_psum"), sem("merge_sb"), sem("merge_rows")
        xn_done, ln_step, sd_done = sem("xn_done"), sem("ln_step"), sem("sd_done")
        ln_rstd, ln_done = sem("ln_rstd"), sem("ln_done")
        lnT_psum, xT_hi, xT_lo = sem("lnT_psum"), sem("xT_hi"), sem("xT_lo")
        gates_psum, gates_sb, gates_rows = sem("gates_psum"), sem("gates_sb"), sem("gates_rows")
        top_step, diff_done, exp_done = sem("top_step"), sem("diff_done"), sem("exp_done")
        chosen_done, ranks, rank_step, slots_done = sem("chosen_done"), sem("ranks"), sem("rank_step"), sem("slots_done")
        scatters, scattered, table_step, tables = sem("scatters"), sem("scattered"), sem("table_step"), sem("tables")
        rows_in = [sem(f"rows_in{i}") for i in range(WR)]
        weights_in = [sem(f"weights_in{i}") for i in range(WR)]
        t_turned, t_xhi, t_xlo, t_up, t_relu = sem("t_turned"), sem("t_xhi"), sem("t_xlo"), sem("t_up"), sem("t_relu")
        t_hi, t_lo, t_down, t_y, t_rows = sem("t_hi"), sem("t_lo"), sem("t_down"), sem("t_y"), sem("t_rows")
        t_out = sem("t_out")
        root_ready = sem("root_ready")
        t_whi, t_wlo_pool, t_wlo_dve = ([sem(f"t_w{m}{part}") for m in ("up", "down")]
                                        for part in ("hi", "lo_pool", "lo_dve"))
        t_stored = [sem(f"t_stored{i}") for i in range(2)]
        kept_in = [sem(f"kept_in{i}") for i in range(2)]
        gather_in = [[sem(f"gather_in{j}_{i}") for i in range(TOP)] for j in range(BLOCKS)]
        sum_step, summed = sem("sum_step"), sem("summed")
        locate_step, located = sem("locate_step"), sem("located")
        out_dma = sem("out_dma")

        LN_STEPS, TOP_STEPS, RANK_STEPS = 8, 5, 3

        def wait(eng, s, value):
            if not isinstance(value, int) or value > 0:
                eng.wait_ge(s, value)

        def at_block(t, j):
            return t[j] if isinstance(j, int) else t[bass.ds(j, 1)].rearrange("o p n -> (o p) n")

        def bodies(eng, body):
            body(0, 0, plan(0))
            body(1, 1, plan(1))
            with eng.Fori(1, GROUP_BLOCKS[0] // 2) as k:
                for par in range(2):
                    body(2 * k + par, par, plan(2))
            for b in range(GROUP_BLOCKS[0], BLOCKS + 1):
                body(b, b % 2, plan(b))

        def tile_turn(i, returned, turned, main, former, ahead_first=False):
            def has(k):
                return not isinstance(i, int) or 0 <= i + k < ALL_TILES

            if ahead_first and has(1):
                turned(i + 1)
            if has(-2):
                returned(i - 2)
            if not ahead_first and has(1):
                turned(i + 1)
            if has(0):
                main(i)
            if has(-1):
                former(i - 1)

        def weights_low(eng, m, i, slot):
            eng.wait_ge(t_whi[m], i + 1)
            eng.tensor_tensor(wsplit[m][:, slot % 2, 1, :], wbuf[:, slot, m * HID:(m + 1) * HID],
                              f(wsplit[m][:, slot % 2, 0, :]), ALU.subtract)\
                .then_inc(t_wlo_pool[m] if by_pool(i) else t_wlo_dve[m], 1)

        def wait_weights(eng, m, i):
            if by_pool(i):
                eng.wait_ge(t_wlo_pool[m], i + 1)
            else:
                eng.wait_ge(t_wlo_dve[m], i + 1 - POOL_TILES)

        def of_ring(i, slot):
            return i // WR + 1 if isinstance(i, int) else (i - slot) // WR + 1

        def by_pool(i):
            return isinstance(i, int) and i < POOL_TILES

        def group(i):
            return 0 if isinstance(i, int) and i < FIRST_TILE[1] else 1

        def last_tiles(eng, turn):
            lo, hi = FIRST_TILE[1], ALL_TILES
            for i in range(lo, lo + 2):
                turn(i, i % WR)
            with eng.Fori(0, (hi - lo) // WR - 1) as k:
                for u in range(WR):
                    turn(WR * k + (lo + 2 + u), (lo + 2 + u) % WR)
            for i in range(hi - 2, hi + 2):
                turn(i, i % WR)

        block = ctx.enter_context(nc.Block())

        @block.sync
        def _(sp):
            def load_x(q):
                if q >= 2:
                    sp.wait_ge(x_lo, q - 1)
                    sp.wait_ge(x2_lo, q - 1)
                sp.dma_start(th[:, q % 2, :], x[q]).then_inc(x_in[q % 2], 16)
                sp.dma_start(rawx2[:, q % 2, :], x2[q]).then_inc(x2_in[q % 2], 16)

            def load_adj(b, c):
                wait(sp, adj_lo, KT * b + KC * (c - RAW) + KC)
                sp.dma_start(raw[:, c % RAW, :], adj[b, c] if isinstance(b, int) else
                             adj[bass.ds(b, 1), c].rearrange("o p n -> (o p) n")).then_inc(raw_in[c % RAW], 16)

            def tile_rows(base):
                return base.rearrange("(p a) d -> p (a d)", a=TA)

            def load_rows(i, slot, g):
                at = sp.value_load(tab[g][0:1, 0, i_of(i, g)], min_val=0, max_val=E * STRIDE[g] - TS)
                wait(sp, t_turned, i - WR + 1)
                sp.dma_start(xr[:, slot, :], tile_rows(xs[g][bass.ds(at, TS), :])).then_inc(rows_in[slot], 16)

            def load_weights(i, slot, g):
                e = sp.value_load(tab[g][0:1, 1, i_of(i, g)], min_val=0, max_val=E - 1)
                wait(sp, t_y, i - WR + 1)
                sp.dma_start(wbuf[:, slot, :], wraw[bass.ds(e, 1)].rearrange("o p n -> (o p) n"))\
                    .then_inc(weights_in[slot], 16)

            def i_of(i, g):
                return slice(i - FIRST_TILE[g], i - FIRST_TILE[g] + 1) if isinstance(i, int) \
                    else bass.ds(i - FIRST_TILE[g], 1)

            def store_rows(i, slot, g):
                sp.wait_ge(t_out, i + 1)
                k = i - FIRST_TILE[g]
                dst = ys[g][k * TS:k * TS + TS, :] if isinstance(i, int) else ys[g][bass.ds(k * TS, TS), :]
                sp.dma_start(tile_rows(dst), tyr[:, slot % 2, :]).then_inc(t_stored[slot % 2], 16)

            def group_ready(g):
                sp.wait_ge(tables, g + 1)
                sp.wait_ge(scattered, 16 * TOP * JT * (GROUP_BLOCKS[0] if g == 0 else BLOCKS))
                sp.wait_ge(zero_out, 16 * E * (g + 1))

            def tiles(i, slot):
                if not isinstance(i, int) or i + 2 < ALL_TILES:
                    if isinstance(i, int) and i + 2 == FIRST_TILE[1]:
                        group_ready(1)
                    load_rows(i + 2, (slot + 2) % WR, group(i + 2))
                    load_weights(i + 2, (slot + 2) % WR, group(i + 2))
                if not isinstance(i, int) or i >= 2:
                    store_rows(i - 2, (slot - 2) % WR, group(i - 2))

            load_x(0)
            for c in range(2):
                load_adj(0, c)
            sp.dma_start(smallS[:, :], small).then_inc(small_in, 16)
            sp.dma_start(wgS[:, :], wg).then_inc(small_in, 16)
            load_x(1)
            sp.dma_start(stage_w[:, :], wsm).then_inc(w_in, 16)
            for c in range(2, NC):
                load_adj(0, c)
                if c % 2 == 0 and 2 + (c - 2) // 2 < BLOCKS:
                    load_x(2 + (c - 2) // 2)
            for c in range(RAW):
                load_adj(1, c)

            def body(b, par, turns):
                if isinstance(b, int) and b == 0:
                    return
                for t, (g, _, stages, tile) in enumerate(turns):
                    if g is not None and g % KC == 0 and g // KC + RAW < NC:
                        load_adj(b, g // KC + RAW)
                    elif g is not None and g % KC == 0 and (not isinstance(b, int) or b < BLOCKS - 1):
                        load_adj(b + 1, g // KC + RAW - NC)
                    if t == 2:
                        wait(sp, xn_done, b - 1)
                        sp.dma_start(xres[:, :], at_block(x, b - 1)).then_inc(xres_in, 16)
                    if isinstance(b, int) and b == BLOCKS - 1 and t == FIRST_STEP - 3:
                        group_ready(0)
                        for i in range(2):
                            load_rows(i, i, 0)
                            load_weights(i, i, 0)
                    if tile is not None:
                        tiles(tile, tile % WR)
                    if g == 28 or (g is None and "close" in stages):
                        sp.wait_ge(slots_done, b)
                        sp.dma_start(at_block(keepd, b - 1), keep[:, :]).then_inc(keep_out, 16)

            bodies(sp, body)
            last_tiles(sp, tiles)
            for j in range(BLOCKS):
                sp.wait_ge(summed, j + 1)
                sp.dma_start(out[j], kept[:, j, 0:NB]).then_inc(out_dma, 16)
            sp.wait_ge(out_dma, 16 * BLOCKS)

        @block.gpsimd
        def _(pool):
            def triangle(dst, compare, step):
                nc.gpsimd.affine_select(out=dst, in_=dst, compare_op=compare, fill=1.0, base=0, pattern=[[step, P]],
                                        channel_multiplier=-step).then_inc(consts, 1)

            nc.gpsimd.memset(ident[:, :], 0.0).then_inc(const_step, 1)
            nc.gpsimd.memset(earlier[:, :], 0.0).then_inc(const_step, 1)
            nc.gpsimd.memset(zero[:, :], 0.0).then_inc(const_step, 1)
            nc.gpsimd.memset(ones[:, :], 1.0).then_inc(const_step, 1)
            nc.gpsimd.memset(upto[:, :, :], 1.0).then_inc(const_step, 1)
            pool.wait_ge(const_step, 5)
            triangle(ident[:, :], ALU.not_equal, -1)
            nc.gpsimd.affine_select(out=earlier[:, :], in_=earlier[:, :], compare_op=ALU.is_ge, fill=1.0, base=0,
                                    pattern=[[-1, P]], channel_multiplier=1).then_inc(consts, 1)
            nc.gpsimd.affine_select(out=upto[:, :, :], in_=upto[:, :, :], compare_op=ALU.is_ge, fill=0.0, base=0,
                                    pattern=[[1, E], [-1, E]], channel_multiplier=0).then_inc(consts, 1)

            def counting(dst, pattern):
                nc.gpsimd.iota(dst, pattern=pattern, base=0, channel_multiplier=0,
                               allow_small_or_imprecise_dtypes=True).then_inc(consts, 1)

            counting(iota[:, :, :], [[0, JT], [1, E]])
            for g in range(2):
                counting(bases[g][:, :], [[STRIDE[g], E]])
            counting(nextslot[:, :], [[STRIDE[0], E]])
            counting(steps_of[:, :, :], [[0, E], [TS, MT]])
            counting(tilei[:, :], [[1, TILES[0]]])

            def x2_low(q):
                pool.wait_ge(x_hi, 2 * q + 1)
                nc.gpsimd.tensor_tensor(Xl[:, JT * q:JT * q + JT, D:2 * D], rows(rawx2[:, q % 2, :]),
                                        f(Xh[:, JT * q:JT * q + JT, D:2 * D]), ALU.subtract).then_inc(x2_lo, 1)

            def x_low(q):
                pool.wait_ge(x_hi, 2 * q + 2)
                nc.gpsimd.tensor_tensor(Xl[:, JT * q:JT * q + JT, 0:D], rows(th[:, q % 2, :]),
                                        f(Xh[:, JT * q:JT * q + JT, 0:D]), ALU.subtract).then_inc(x_lo, 1)

            def scatter(j, g, pieces=range(TOP * JT)):
                if 0 in pieces:
                    pool.wait_ge(slots_done, j + 1)
                    pool.sem_inc(scatters, 1)
                for p in pieces:
                    at = p % JT * D
                    pool.indirect_dma_start(
                        out=xs[g][:, :], in_=lnr[:, at:at + D], in_offset=None,
                        out_offset=bass.IndirectOffsetOnAxis(ap=slots[:, p:p + 1], axis=0)).then_inc(scattered, 16)

            def fill_behind(g):
                pool.wait_ge(ends_known, g + 1)
                for e in range(E):
                    at = pool.value_load(ends_at[g][0:1, e:e + 1], min_val=0, max_val=E * STRIDE[g] - TS)
                    pool.dma_start(xs[g][bass.ds(at, TS), :].rearrange("(p a) d -> p a d", a=TA),
                                 zero[:, :].rearrange("p (o d) -> p o d", o=1).to_broadcast([P, TA, D]))\
                        .then_inc(zero_out, 16)

            def load_kept(j):
                pool.wait_ge(keep_out, 16 * (j + 1))
                pool.dma_start(kept[:, j, :], keepd[j]).then_inc(kept_in[0 if j < GROUP_BLOCKS[0] else 1], 16)

            def gather(g):
                for k in range(2):
                    pool.wait_ge(t_stored[k], 16 * (FIRST_TILE[g] + TILES[g]) // 2)
                pool.wait_ge(located, g + 1)
                first = g * GROUP_BLOCKS[0]
                for j in range(first, first + GROUP_BLOCKS[g]):
                    for i in range(TOP * JT):
                        pool.indirect_dma_start(
                            out=gathered[:, j, i, :], out_offset=None, in_=ys[g][:, :],
                            in_offset=bass.IndirectOffsetOnAxis(ap=resrow[:, j, i:i + 1], axis=0)
                        ).then_inc(gather_in[j][i // JT], 16)

            def weights(i):
                if by_pool(i + 1):
                    weights_low(pool, 0, i + 1, (i + 1) % WR)
                if by_pool(i):
                    weights_low(pool, 1, i, i % WR)

            x2_low(0)
            for q in range(1, BLOCKS):
                x2_low(q)
                x_low(q)
            pool.wait_ge(w_hi, 1)
            nc.gpsimd.tensor_tensor(Wsl[:, :], stage_w[:, :], f(Wsh[:, :]), ALU.subtract).then_inc(w_lo, 1)
            scatter(0, 0)
            with pool.Fori(1, GROUP_BLOCKS[0] - 1) as j:
                scatter(j, 0)
            scatter(GROUP_BLOCKS[0] - 1, 0)
            fill_behind(0)
            for b in range(BLOCKS - 1, BLOCKS + 1):
                pieces = []
                for t, (_, _, stages, tile) in enumerate(plan(b)):
                    if tile == 0:
                        weights_low(pool, 0, 0, 0)
                    if tile is not None:
                        weights(tile)
                    if b == BLOCKS and t == 0:
                        pool.wait_ge(gnn_done, KT * BLOCKS)
                    if b == BLOCKS and t < GROUP_BLOCKS[0]:
                        load_kept(t)
                    if "rank" in stages:
                        pieces = list(range(TOP * JT))
                    n = 1 if b < BLOCKS else TOP * JT
                    if pieces:
                        scatter(b - 1, 1, pieces[0:n])
                    pieces = pieces[n:]
            fill_behind(1)
            for j in range(GROUP_BLOCKS[0], BLOCKS):
                load_kept(j)
            for g in range(2):
                gather(g)

        @block.tensor
        def _(pe):
            def three(ps, wh, wl, ih, il, start, stop):
                pe.matmul(ps, wh, ih, start=start, stop=False)
                pe.matmul(ps, wh, il, start=False, stop=False)
                return pe.matmul(ps, wl, ih, start=False, stop=stop)

            def gnn(b, par, s):
                if isinstance(b, int) and b == 0 and s % 4 == 0:
                    pe.wait_ge(x_lo, s // 4 + 1)
                    pe.wait_ge(x2_lo, s // 4 + 1)
                pe.wait_ge(adj_lo, KT * b + s + 1)
                for half in range(2):
                    if s == 0 and not (isinstance(b, int) and b < 2):
                        pe.wait_ge(h_split, 8 * (b - 2) + half + 1)
                    at = slice(half * D, half * D + D)
                    last = three(sums[par][half][:, :], Xh[:, s, at], Xl[:, s, at], Ah[:, s % RING, :],
                                 Al[:, s % RING, :], s == 0, s == KT - 1)
                    if s == KT - 1 and half == 0:
                        last.then_inc(acc_done, 1)
                last.then_inc(gnn_done, 1)

            def turn_rows(dst, src):
                for t in range(JT):
                    at = slice(t * P, t * P + P)
                    last = pe.transpose(dst[:, at], src[:, at], ident[:, :])
                return last

            def stage(name, j):
                if name.startswith("layer"):
                    l = int(name[5:])
                    for half in range(2):
                        pe.wait_ge(h_split, 8 * j + 2 * (l - 1) + half + 1)
                        at = slice((half * LAYERS + l - 1) * D, (half * LAYERS + l) * D)
                        three(lay[half][:, :], Wsh[:, at], Wsl[:, at], lh[:, half, :], ll[:, half, :], True, True)\
                            .then_inc(lay_done, 1)
                elif name == "merge":
                    for half in range(2):
                        pe.wait_ge(h_split, 8 * j + 6 + half + 1)
                        at = slice((2 * LAYERS + half) * D, (2 * LAYERS + half + 1) * D)
                        last = three(lay[0][:, :], Wsh[:, at], Wsl[:, at], lh[:, half, :], ll[:, half, :],
                                     half == 0, half == 1)
                    last.then_inc(merge_psum, 1)
                elif name == "rows":
                    pe.wait_ge(merge_sb, j + 1)
                    turn_rows(lay[1], hbuf[:, 0, :]).then_inc(merge_rows, 1)
                elif name == "normT":
                    pe.wait_ge(ln_done, BLOCKS + j + 1)
                    turn_rows(lay[0], lnr).then_inc(lnT_psum, 1)
                elif name == "gates":
                    pe.wait_ge(xT_lo, j + 1)
                    three(lay[1][0:E, :], wgh[:, :], wgl[:, :], xTh[:, :], xTl[:, :], True, True)\
                        .then_inc(gates_psum, 1)
                elif name == "top_a":
                    pe.wait_ge(gates_sb, j + 1)
                    for t in range(JT):
                        last = pe.matmul(lay[0][:, t * E:t * E + E], hbuf[0:E, 1, t * P:t * P + P],
                                         ident[0:E, 0:E], start=True, stop=True)
                    last.then_inc(gates_rows, 1)
                elif name == "rank":
                    pe.wait_ge(chosen_done, j + 1)
                    pe.matmul(lay[1][:, 0:(JT + 1) * E], earlier[:, :], chosen[:, :], start=True, stop=False)
                    for t in range(JT):
                        m = JT - t
                        src = chosen[:, t * E:t * E + E].rearrange("p (o e) -> p o e", o=1).to_broadcast([P, m, E])
                        last = pe.matmul(lay[1][:, (t + 1) * E:(JT + 1) * E].rearrange("p (o e) -> p o e", e=E),
                                         ones[:, :], src, start=False, stop=(t == JT - 1))
                    last.then_inc(ranks, 1)

            def turn_tile(i, slot):
                pe.wait_ge(rows_in[slot], 16 * of_ring(i, slot))
                wait(pe, t_xlo, i)
                for a in range(TA):
                    at = slice(a * P, a * P + P)
                    last = pe.transpose(tin[:, at], xr[:, slot, at], ident[:, :])
                last.then_inc(t_turned, 1)

            def up_tile(i, slot):
                wait_weights(pe, 0, i)
                pe.wait_ge(t_xlo, i + 1)
                for pair in range(2):
                    wait(pe, t_relu, 2 * i - 1 + pair)
                    for half in range(2):
                        c = 2 * pair + half
                        last = three(upP[pair][:, half * TS:half * TS + TS],
                                     wsplit[0][:, slot % 2, 0, c * P:c * P + P],
                                     wsplit[0][:, slot % 2, 1, c * P:c * P + P],
                                     tTh[:, slot % 2, :], tTl[:, slot % 2, :], True, True)
                    last.then_inc(t_up, 1)

            def down_tile(i, slot):
                wait_weights(pe, 1, i)
                pe.wait_ge(t_lo, 2 * i + 2)
                wait(pe, t_out, i)
                for c in range(HC):
                    hid = (slice(None), slot % 2, c // 2, slice((c % 2) * TS, (c % 2) * TS + TS))
                    last = three(ty[:, 0:TS], wsplit[1][:, slot % 2, 0, c * P:c * P + P],
                                 wsplit[1][:, slot % 2, 1, c * P:c * P + P], tHh[hid], tHl[hid],
                                 c == 0, c == HC - 1)
                last.then_inc(t_down, 1)

            def return_tile(i, slot):
                pe.wait_ge(t_y, i + 1)
                for a in range(TA):
                    last = pe.transpose(ty[:, TS + a * P:TS + a * P + P], tyT[:, slot % 2, a * P:a * P + P], ident[:, :])
                last.then_inc(t_rows, 1)

            def tiles(i, slot):
                tile_turn(i, lambda k: return_tile(k, (slot - 2) % WR), lambda k: turn_tile(k, (slot + 1) % WR),
                          lambda k: up_tile(k, slot), lambda k: down_tile(k, (slot - 1) % WR), ahead_first=True)

            def body(b, par, turns):
                if isinstance(b, int) and b == 1:
                    pe.wait_ge(w_lo, 1)
                    pe.wait_ge(small_split, 3)
                for g, _, stages, tile in turns:
                    for name in stages:
                        if name not in ("h0", "norm_a", "norm_b", "top_b", "close"):
                            stage(name, b - 1)
                    if tile == 0:
                        turn_tile(0, 0)
                    if g is not None:
                        gnn(b, par, g)
                    if tile is not None:
                        tiles(tile, tile % WR)

            pe.wait_ge(consts, 9)
            bodies(pe, body)
            last_tiles(pe, tiles)

        @block.scalar
        def _(act):
            def high(dst, src):
                return nc.scalar.activation(dst, src, ACT.Copy)

            def adj_high(b, k):
                c, slot = k // KC, (k // KC) % RAW
                act.wait_ge(raw_in[slot], 16 * (NC // RAW * b + c // RAW + 1))
                wait(act, gnn_done, KT * b + k - RING + 1)
                high(Ah[:, k % RING, :], raw[:, slot, (k % KC) * NB:(k % KC + 1) * NB]).then_inc(adj_hi, 1)

            def x_high(q, part):
                at = slice(JT * q, JT * q + JT)
                if part == 0:
                    act.wait_ge(x2_in[q % 2], 16 * (q // 2 + 1))
                    high(Xh[:, at, D:2 * D], rows(rawx2[:, q % 2, :])).then_inc(x_hi, 1)
                    if q == 0:
                        act.wait_ge(root_ready, 1)
                    act.wait_ge(ln_step, LN_STEPS * q + 4)
                    act.activation(nrm[:, 1, :], nrm[:, 0, :], ACT.Sqrt).then_inc(sd_done, 1)
                elif part == 1:
                    act.wait_ge(ln_done, q + 1)
                    high(Xh[:, at, 0:D], rows(th[:, q % 2, :])).then_inc(x_hi, 1)

            def weights_high(m, i, slot):
                act.wait_ge(weights_in[slot], 16 * of_ring(i, slot))
                if m == 0:
                    wait(act, t_up, 2 * (i - 1))
                else:
                    wait(act, t_down, i - 1)
                high(wsplit[m][:, slot % 2, 0, :], wbuf[:, slot, m * HID:(m + 1) * HID]).then_inc(t_whi[m], 1)

            def stage(name, j, par):
                if name == "h0":
                    wait(act, merge_psum, j)
                    for half in range(2):
                        if half == 0:
                            act.wait_ge(acc_done, j + 1)
                        else:
                            act.wait_ge(gnn_done, KT * j + KT)
                        nc.scalar.activation(lh[:, half, :], sums[par][half][:, :], ACT.Copy,
                                             scale=eps1p[:, half:half + 1]).then_inc(h_hi, 1)
                elif name.startswith("layer"):
                    l = int(name[5:])
                    for half in range(2):
                        act.wait_ge(lay_done, 6 * j + 2 * (l - 1) + half + 1)
                        bias = smallS[:, C_CONV_B + half * LAYERS + l - 1:C_CONV_B + half * LAYERS + l]
                        nc.scalar.activation(hbuf[:, half, :], lay[half][:, :], ACT.Relu, bias=bias)
                        nc.scalar.activation(lh[:, half, :], lay[half][:, :], ACT.Relu, bias=bias)\
                            .then_inc(h_hi, 1)
                elif name == "merge":
                    act.wait_ge(merge_psum, j + 1)
                    nc.scalar.activation(hbuf[:, 0, :], lay[0][:, :], ACT.Identity,
                                         bias=smallS[:, C_BM:C_BM + 1]).then_inc(merge_sb, 1)
                elif name == "norm_b":
                    act.wait_ge(ln_step, LN_STEPS * (BLOCKS + j) + 4)
                    act.activation(nrm[:, 1, :], nrm[:, 0, :], ACT.Sqrt).then_inc(sd_done, 1)
                elif name == "normT":
                    act.wait_ge(lnT_psum, j + 1)
                    wait(act, gates_psum, j)
                    high(xTh[:, :], lay[0][:, :]).then_inc(xT_hi, 1)
                elif name == "gates":
                    act.wait_ge(gates_psum, j + 1)
                    nc.scalar.activation(hbuf[0:E, 1, :], lay[1][0:E, :], ACT.Identity,
                                         bias=smallS[0:E, C_BG:C_BG + 1]).then_inc(gates_sb, 1)
                elif name == "top_b":
                    act.wait_ge(diff_done, j + 1)
                    nc.scalar.activation(prob[:, 1, :], prob[:, 0, :], ACT.Exp).then_inc(exp_done, 1)

            def turned_tile(i, slot):
                act.wait_ge(t_turned, i + 1)
                wait(act, t_up, 2 * (i - 1))
                high(tTh[:, slot % 2, :], tin[:, 0:TS]).then_inc(t_xhi, 1)
                weights_high(0, i, slot)

            def relu_tile(i, slot):
                for pair in range(2):
                    wait(act, t_lo, 2 * (i - 1) + pair + 1)
                    act.wait_ge(t_up, 2 * i + pair + 1)
                    for half in range(2):
                        c, at = 2 * pair + half, slice(half * TS, half * TS + TS)
                        last = nc.scalar.activation(th[:, pair, at], upP[pair][:, at], ACT.Relu,
                                                    bias=wbuf[:, slot, WS + c:WS + c + 1])
                    last.then_inc(t_relu, 1)
                weights_high(1, i, slot)

            def return_tile(i, slot):
                par = slot % 2
                wait(act, t_stored[par], 8 * (i - par))
                act.wait_ge(t_rows, i + 1)
                nc.scalar.activation(tyr[:, par, :], ty[:, TS:2 * TS], ACT.Copy).then_inc(t_out, 1)

            def sum_tile(i, slot):
                wait(act, t_rows, i - 1)
                act.wait_ge(t_down, i + 1)
                nc.scalar.activation(tyT[:, slot % 2, :], ty[:, 0:TS], ACT.Identity,
                                     bias=wbuf[:, slot, WS + HC:WS + HC + 1]).then_inc(t_y, 1)

            def tiles(i, slot):
                tile_turn(i, lambda k: return_tile(k, (slot - 2) % WR), lambda k: turned_tile(k, (slot + 1) % WR),
                          lambda k: relu_tile(k, slot), lambda k: sum_tile(k, (slot - 1) % WR), ahead_first=True)

            def body(b, par, turns):
                first = isinstance(b, int) and b == 0
                for g, split, stages, tile in turns:
                    for name in stages:
                        stage(name, b - 1, 1 - par)
                    if tile == 0:
                        turned_tile(0, 0)
                    for k in split:
                        adj_high(b, k)
                    if first:
                        for q, part in x_parts(g):
                            if part != 1:
                                x_high(q, part // 2)
                        if g == SPLIT_W:
                            act.wait_ge(small_in, 32)
                            high(wgh[:, :], wgS[:, :]).then_inc(small_split, 1)
                            act.wait_ge(w_in, 16)
                            high(Wsh[:, :], stage_w[:, :]).then_inc(w_hi, 1)
                    if tile is not None:
                        tiles(tile, tile % WR)

            act.wait_ge(const_step, 3)
            act.activation(nrm[:, 1, :], zero[:, 0:JT], ACT.Sqrt).then_inc(root_ready, 1)
            x_high(0, 0)
            for k in range(AHEAD - 1):
                adj_high(0, k)
            x_high(0, 1)
            adj_high(0, AHEAD - 1)
            bodies(act, body)
            last_tiles(act, tiles)

        @block.vector
        def _(dve):
            def low(dst, src, hi):
                return nc.vector.tensor_tensor(dst, src, f(hi), ALU.subtract)

            def adj_low(b, k):
                dve.wait_ge(adj_hi, KT * b + k + 1)
                low(Al[:, k % RING, :], raw[:, (k // KC) % RAW, (k % KC) * NB:(k % KC + 1) * NB],
                    Ah[:, k % RING, :]).then_inc(adj_lo, 1)

            def variance(use, src):
                base = LN_STEPS * use
                for t in range(JT):
                    last = nc.vector.bn_stats(stats[:, t, :], src[:, t * D:t * D + D])
                last.then_inc(ln_step, 1)
                dve.wait_ge(ln_step, base + 1)
                nc.vector.tensor_tensor(mom[:, 0, :], stats[:, :, 1], stats[:, :, 4], ALU.add)
                nc.vector.tensor_tensor(mom[:, 1, :], stats[:, :, 1], stats[:, :, 4], ALU.subtract)
                nc.vector.tensor_tensor(mom[:, 2, :], stats[:, :, 2], stats[:, :, 5], ALU.add).then_inc(ln_step, 1)
                dve.wait_ge(ln_step, base + 2)
                nc.vector.tensor_scalar(mean[:, :], mom[:, 0, :], 0.5, None, ALU.mult)
                nc.vector.tensor_tensor(mom[:, 3, :], mom[:, 1, :], mom[:, 1, :], ALU.mult)
                nc.vector.tensor_scalar(mom[:, 4, :], mom[:, 2, :], 1.0 / D, EPS, ALU.mult, ALU.add)\
                    .then_inc(ln_step, 1)
                dve.wait_ge(ln_step, base + 3)
                nc.vector.scalar_tensor_tensor(out=nrm[:, 0, :], in0=mom[:, 3, :], scalar=0.25, in1=mom[:, 4, :],
                                               op0=ALU.mult, op1=ALU.add).then_inc(ln_step, 1)

            def normalise(use, dst, src):
                base = LN_STEPS * use
                dve.wait_ge(sd_done, use + 1)
                nc.vector.reciprocal(nrm[:, 2, :], nrm[:, 1, :]).then_inc(ln_step, 1)
                dve.wait_ge(ln_step, base + 5)
                nc.vector.tensor_tensor(nrm[:, 3, :], nrm[:, 2, :], nrm[:, 2, :], ALU.mult).then_inc(ln_step, 1)
                dve.wait_ge(ln_step, base + 6)
                nc.vector.tensor_tensor(nrm[:, 4, :], nrm[:, 3, :], nrm[:, 0, :], ALU.mult).then_inc(ln_step, 1)
                dve.wait_ge(ln_step, base + 7)
                nc.vector.tensor_scalar(nrm[:, 3, :], nrm[:, 4, :], -0.5, 1.5, ALU.mult, ALU.add).then_inc(ln_step, 1)
                dve.wait_ge(ln_step, base + 8)
                nc.vector.tensor_tensor(nrm[:, 5, :], nrm[:, 3, :], nrm[:, 2, :], ALU.mult).then_inc(ln_rstd, 1)
                dve.wait_ge(ln_rstd, use + 1)
                for t in range(JT):
                    at = slice(t * D, t * D + D)
                    last = nc.vector.tensor_scalar(dst[:, at], src[:, at], mean[:, t:t + 1], nrm[:, 5, t:t + 1],
                                                   ALU.subtract, ALU.mult)
                last.then_inc(ln_done, 1)

            def x_prepare(q, part):
                at = slice(JT * q, JT * q + JT)
                if part == 0:
                    dve.wait_ge(x_in[q % 2], 16 * (q // 2 + 1))
                    variance(q, th[:, q % 2, :])
                elif part == 1:
                    normalise(q, th[:, q % 2, :], th[:, q % 2, :])
                else:
                    dve.wait_ge(x_hi, 2 * q + 2)
                    low(Xl[:, at, 0:D], rows(th[:, q % 2, :]), Xh[:, at, 0:D]).then_inc(x_lo, 1)

            def stage(name, j, par):
                if name == "h0":
                    for half in range(2):
                        dve.wait_ge(h_hi, 8 * j + half + 1)
                        nc.vector.scalar_tensor_tensor(out=ll[:, half, :], in0=sums[par][half][:, :],
                                                       scalar=eps1p[:, half:half + 1], in1=f(lh[:, half, :]),
                                                       op0=ALU.mult, op1=ALU.subtract).then_inc(h_split, 1)
                elif name.startswith("layer"):
                    l = int(name[5:])
                    for half in range(2):
                        dve.wait_ge(h_hi, 8 * j + 2 * l + half + 1)
                        low(ll[:, half, :], hbuf[:, half, :], lh[:, half, :]).then_inc(h_split, 1)
                elif name == "rows":
                    dve.wait_ge(merge_rows, j + 1)
                    dve.wait_ge(xres_in, 16 * j + 16)
                    wait(dve, keep_out, 16 * j)
                    nc.vector.tensor_tensor(keep[:, 0:NB], lay[1][:, :], xres[:, :], ALU.add).then_inc(xn_done, 1)
                elif name == "norm_a":
                    dve.wait_ge(xn_done, j + 1)
                    variance(BLOCKS + j, keep)
                elif name == "norm_b":
                    wait(dve, scattered, 16 * TOP * JT * j)
                    normalise(BLOCKS + j, lnr, keep)
                elif name == "normT":
                    dve.wait_ge(xT_hi, j + 1)
                    low(xTl[:, :], lay[0][:, :], xTh[:, :]).then_inc(xT_lo, 1)
                elif name == "top_a":
                    base = TOP_STEPS * j
                    dve.wait_ge(gates_rows, j + 1)
                    scores = lay[0][:, 0:JT * E].rearrange("p (j e) -> p j e", j=JT)
                    nc.vector.tensor_copy(gS[:, :, :], scores)
                    for t in range(JT):
                        last = nc.vector.max(top[:, t, :], scores[:, t, :])
                    last.then_inc(top_step, 1)
                    dve.wait_ge(top_step, base + 1)
                    nc.vector.tensor_tensor(prob[:, 0, :], top[:, :, 1], top[:, :, 0], ALU.subtract)\
                        .then_inc(diff_done, 1)
                    for t in range(JT):
                        last = nc.vector.max_index(topi[:, t, :], top[:, t, :], gS[:, t, :])
                    last.then_inc(top_step, 1)
                    dve.wait_ge(top_step, base + 2)
                    nc.vector.tensor_copy(topf[:, :, :], topi[:, :, 0:2]).then_inc(top_step, 1)
                elif name == "top_b":
                    base = TOP_STEPS * j
                    dve.wait_ge(exp_done, j + 1)
                    nc.vector.tensor_scalar(prob[:, 2, :], prob[:, 1, :], 1.0, None, ALU.add).then_inc(top_step, 1)
                    dve.wait_ge(top_step, base + 4)
                    nc.vector.reciprocal(keep_p[:, 0, :], prob[:, 2, :])
                    for i in range(TOP):
                        last = nc.vector.tensor_tensor(by_expert(chose[:, i, :]), iota[:, :, :],
                                                       topf[:, :, i:i + 1].to_broadcast([P, JT, E]), ALU.is_equal)
                    last.then_inc(top_step, 1)
                    dve.wait_ge(top_step, base + 5)
                    nc.vector.tensor_tensor(keep_p[:, 1, :], prob[:, 1, :], keep_p[:, 0, :], ALU.mult)
                    nc.vector.tensor_tensor(chosen[:, 0:JT * E], chose[:, 0, :], chose[:, 1, :], ALU.add)\
                        .then_inc(chosen_done, 1)
                elif name == "rank":
                    base = RANK_STEPS * j
                    dve.wait_ge(ranks, j + 1)
                    nc.vector.tensor_tensor(place[:, :, :], by_expert(lay[1][:, 0:JT * E]),
                                            nextslot[:, :].rearrange("p (o e) -> p o e", o=1)
                                            .to_broadcast([P, JT, E]), ALU.add).then_inc(rank_step, 1)
                    dve.wait_ge(rank_step, base + 1)
                    nc.vector.tensor_tensor(nextslot[:, :], lay[1][:, JT * E:(JT + 1) * E], nextslot[:, :], ALU.add)
                    for i in range(TOP):
                        last = nc.vector.tensor_tensor(by_expert(picked[:, i, :]), place[:, :, :],
                                                       by_expert(chose[:, i, :]), ALU.mult)
                    last.then_inc(rank_step, 1)
                    dve.wait_ge(rank_step, base + 2)
                    nc.vector.tensor_reduce(keep_slot, picked[:, :, :].rearrange("p i (j e) -> p (i j) e", e=E),
                                            AX.X, ALU.add).then_inc(rank_step, 1)
                    dve.wait_ge(rank_step, base + 3)
                    nc.vector.tensor_copy(slots[:, :], keep_slot).then_inc(slots_done, 1)
                elif name == "close":
                    close(0 if j < GROUP_BLOCKS[0] else 1)

            table_steps = [0]

            def close(g):
                n = TILES[g]

                def then(last):
                    table_steps[0] += 1
                    last.then_inc(table_step, 1)
                    dve.wait_ge(table_step, table_steps[0])

                def each(i):
                    return tt[:, i, 0:n]

                def wide(ap, shape):
                    return ap.rearrange("p (o e) -> p o e", o=1).to_broadcast(shape)

                tokens, tiles_of, ends, shifts = (count[:, i, :] for i in range(4))
                ge, ge_tiles = (by_expert(passed[:, i, 0:n * E]) for i in range(2))
                nc.vector.tensor_copy(ends_at[g][:, :], nextslot[0:1, :]).then_inc(ends_known, 1)
                then(nc.vector.tensor_tensor(tokens, nextslot[:, :], bases[g][:, :], ALU.subtract))
                if g == 0:
                    nc.vector.tensor_copy(nextslot[:, :], bases[1][:, :])
                then(nc.vector.tensor_tensor(wideM[:, :, :], tokens.rearrange("p (e o) -> p e o", o=1)
                                             .to_broadcast([P, E, MT]), steps_of[:, :, :], ALU.is_gt))
                then(nc.vector.tensor_reduce(tiles_of, wideM[:, :, :], AX.X, ALU.add))
                then(nc.vector.tensor_tensor(wide8[:, :, :], upto[:, :, :], wide(tiles_of, [P, E, E]), ALU.mult))
                then(nc.vector.tensor_reduce(ends, wide8[:, :, :], AX.X, ALU.add))
                nc.vector.tensor_tensor(tokens, ends, tiles_of, ALU.subtract)
                then(nc.vector.tensor_tensor(ge, tilei[:, 0:n].rearrange("p (i o) -> p i o", o=1)
                                             .to_broadcast([1, n, E]), wide(ends[0:1], [1, n, E]), ALU.is_ge))
                nc.vector.scalar_tensor_tensor(out=shifts, in0=tokens, scalar=float(TS), in1=bases[g][:, :],
                                               op0=ALU.mult, op1=ALU.subtract)
                then(nc.vector.tensor_tensor(ge_tiles, ge, wide(tiles_of[0:1], [1, n, E]), ALU.mult))
                nc.vector.tensor_copy(moved[g][:, 0:1], shifts[:, 0:1])
                nc.vector.tensor_tensor(moved[g][:, 1:E], shifts[:, 1:E], shifts[:, 0:E - 1], ALU.subtract)
                nc.vector.tensor_reduce(each(0), ge, AX.X, ALU.add)
                then(nc.vector.tensor_reduce(each(1), ge_tiles, AX.X, ALU.add))
                nc.vector.tensor_scalar(each(2), each(0), float(E), None, ALU.is_lt)
                nc.vector.tensor_scalar(each(4), each(0), float(STRIDE[g]), None, ALU.mult)
                then(nc.vector.tensor_tensor(each(3), tilei[:, 0:n], each(1), ALU.subtract))
                then(nc.vector.tensor_scalar(each(5), each(3), float(TS), None, ALU.mult))
                then(nc.vector.tensor_tensor(each(6), each(4), each(5), ALU.add))
                nc.vector.tensor_tensor(tab[g][:, 0, :], each(6), each(2), ALU.mult)
                nc.vector.tensor_tensor(tab[g][:, 1, :], each(0), each(2), ALU.mult).then_inc(tables, 1)

            def turned_tile(i, slot):
                dve.wait_ge(t_xhi, i + 1)
                low(tTl[:, slot % 2, :], tin[:, 0:TS], tTh[:, slot % 2, :]).then_inc(t_xlo, 1)
                if not by_pool(i):
                    weights_low(dve, 0, i, slot)

            def split_tile(i, slot):
                for pair in range(2):
                    wait(dve, t_down, i - 1)
                    dve.wait_ge(t_relu, 2 * i + pair + 1)
                    nc.vector.tensor_copy(tHh[:, slot % 2, pair, :], th[:, pair, :]).then_inc(t_hi, 1)
                    dve.wait_ge(t_hi, 2 * i + pair + 1)
                    low(tHl[:, slot % 2, pair, :], th[:, pair, :], tHh[:, slot % 2, pair, :]).then_inc(t_lo, 1)
                if not by_pool(i):
                    weights_low(dve, 1, i, slot)

            def tiles(i, slot):
                tile_turn(i, lambda k: None, lambda k: turned_tile(k, (slot + 1) % WR),
                          lambda k: split_tile(k, slot), lambda k: None)

            def locate(g):
                dve.wait_ge(kept_in[g], 16 * GROUP_BLOCKS[g])
                first, n = g * GROUP_BLOCKS[0], GROUP_BLOCKS[g]

                def of_block(i, j):
                    return by_expert(beyond[:, i, j * TOP * JT * E:(j + 1) * TOP * JT * E])

                def wide(ap):
                    return ap.rearrange("p (o e) -> p o e", o=1).to_broadcast([P, TOP * JT, E])

                def slot(j):
                    return kept[:, first + j, NB + TOP * JT:KEEP]

                for j in range(n):
                    last = nc.vector.tensor_tensor(of_block(0, j), slot(j).rearrange("p (i o) -> p i o", o=1)
                                                   .to_broadcast([P, TOP * JT, E]), wide(bases[g][:, :]), ALU.is_ge)
                last.then_inc(locate_step, 1)
                dve.wait_ge(locate_step, 3 * g + 1)
                for j in range(n):
                    last = nc.vector.tensor_tensor(of_block(1, j), of_block(0, j), wide(moved[g][:, :]), ALU.mult)
                last.then_inc(locate_step, 1)
                dve.wait_ge(locate_step, 3 * g + 2)
                for j in range(n):
                    last = nc.vector.tensor_reduce(rowf[:, j, :], of_block(1, j), AX.X, ALU.add)
                last.then_inc(locate_step, 1)
                dve.wait_ge(locate_step, 3 * g + 3)
                for j in range(n):
                    last = nc.vector.tensor_tensor(resrow[:, first + j, :], rowf[:, j, :], slot(j), ALU.add)
                last.then_inc(located, 1)

            def sum_up(j):
                for i in range(TOP):
                    dve.wait_ge(gather_in[j][i], 16 * JT)
                    for t in range(JT):
                        at = slice(t * D, t * D + D)
                        last = nc.vector.scalar_tensor_tensor(
                            out=kept[:, j, at], in0=gathered[:, j, i * JT + t, :],
                            scalar=kept[:, j, NB + i * JT + t:NB + i * JT + t + 1], in1=kept[:, j, at],
                            op0=ALU.mult, op1=ALU.add)
                    if i == 0:
                        last.then_inc(sum_step, 1)
                        dve.wait_ge(sum_step, j + 1)
                last.then_inc(summed, 1)

            def body(b, par, turns):
                for g, split, stages, tile in turns:
                    for name in stages:
                        stage(name, b - 1, 1 - par)
                    if tile == 0:
                        turned_tile(0, 0)
                    if g is None and "gates" in stages:
                        locate(0)
                    for k in split:
                        adj_low(b, k)
                    if isinstance(b, int) and b == 0:
                        for q, part in x_parts(g):
                            if part < 2:
                                x_prepare(q, part)
                        if g == SPLIT_W:
                            dve.wait_ge(small_in, 32)
                            dve.wait_ge(small_split, 1)
                            low(wgl[:, :], wgS[:, :], wgh[:, :]).then_inc(small_split, 1)
                            nc.vector.tensor_scalar(eps1p[:, :], smallS[:, C_EPS:C_EPS + 2], 1.0, 1.0,
                                                    ALU.add, ALU.add).then_inc(small_split, 1)
                    if tile is not None:
                        tiles(tile, tile % WR)

            for part in range(2):
                x_prepare(0, part)
            adj_low(0, 0)
            x_prepare(0, 2)
            for k in range(1, AHEAD):
                adj_low(0, k)
            nc.vector.memset(chosen[:, :], 0.0)
            dve.wait_ge(consts, 9)
            bodies(dve, body)
            locate(1)
            last_tiles(dve, tiles)
            for j in range(BLOCKS):
                sum_up(j)


def kernel(x, adj, L0_gnn_x2, L0_gnn_eps1, L0_gnn_eps2, L0_gnn_W1, L0_gnn_b1, L0_gnn_W2, L0_gnn_b2, L0_gnn_Wm,
           L0_gnn_bm, L0_ffn_Wg, L0_ffn_bg, L0_ffn_W1, L0_ffn_b1, L0_ffn_W2, L0_ffn_b2):
    import numpy as np
    import concourse.bacc as bacc
    from concourse.bass_utils import run_bass_kernel_spmd

    def row_blocks(a):
        return np.ascontiguousarray(np.asarray(a).reshape(BLOCKS, JT, P, D).transpose(0, 2, 1, 3)).reshape(BLOCKS, P, NB)

    adj_l = np.asarray(adj).reshape(BLOCKS, NB, NC, KC, P).transpose(0, 2, 4, 3, 1)
    adj_l = np.ascontiguousarray(adj_l).reshape(BLOCKS, NC, P, KC * NB)
    wm = np.asarray(L0_gnn_Wm)
    wsm = np.concatenate([np.asarray(w)[i].T for w in (L0_gnn_W1, L0_gnn_W2) for i in range(LAYERS)]
                         + [wm[:, 0:D].T, wm[:, D:2 * D].T], axis=1)
    w1 = np.asarray(L0_ffn_W1).transpose(0, 2, 1)
    w2 = np.asarray(L0_ffn_W2).reshape(E, D, HC, P).transpose(0, 3, 2, 1).reshape(E, P, HC * D)
    bset = np.zeros((E, P, BS), np.float32)
    bset[:, :, 0:HC] = np.asarray(L0_ffn_b1).reshape(E, HC, P).transpose(0, 2, 1)
    bset[:, :, HC] = np.asarray(L0_ffn_b2)

    small = np.zeros((P, C_ALL), np.float32)
    small[:, C_EPS] = np.asarray(L0_gnn_eps1)[0]
    small[:, C_EPS + 1] = np.asarray(L0_gnn_eps2)[0]
    small[:, C_CONV_B:C_CONV_B + LAYERS] = np.asarray(L0_gnn_b1).T
    small[:, C_CONV_B + LAYERS:C_CONV_B + 2 * LAYERS] = np.asarray(L0_gnn_b2).T
    small[:, C_BM] = np.asarray(L0_gnn_bm)
    small[0:E, C_BG] = np.asarray(L0_ffn_bg)
    arrays = {
        "adj_l": adj_l, "x_rows": row_blocks(x), "x2_rows": row_blocks(L0_gnn_x2),
        "wsm": np.ascontiguousarray(wsm), "wraw": np.ascontiguousarray(np.concatenate([w1, w2, bset], axis=2)),
        "wg": np.ascontiguousarray(np.asarray(L0_ffn_Wg).T), "small": small,
    }
    nc = bacc.Bacc("TRN2", target_bir_lowering=False, num_devices=1, dynamic_dma_scratch_size=4096)
    args = [nc.dram_tensor(n, a.shape, F32, kind="ExternalInput").ap() for n, a in arrays.items()]
    out = nc.dram_tensor("out_rows", (BLOCKS, P, NB), F32, kind="ExternalOutput").ap()
    keepd = nc.dram_tensor("keepd", (BLOCKS, P, NB + 2 * TOP * JT), F32, kind="Internal").ap()
    xs = [nc.dram_tensor(f"slots{g}", (E * STRIDE[g], D), F32, kind="Internal").ap() for g in range(2)]
    ys = [nc.dram_tensor(f"results{g}", (TS * TILES[g], D), F32, kind="Internal").ap() for g in range(2)]
    gnn_mixture(nc, *args, out, keepd, xs, ys)
    r = run_bass_kernel_spmd(nc, [arrays], core_ids=[0])
    got = np.asarray(r.results[0]["out_rows"])
    return got.reshape(BLOCKS, P, JT, D).transpose(0, 2, 1, 3).reshape(N, D)
```
